# Optimizing a Trainium2 kernel written in Bass

```python
import numpy as np
import jax
import jax.numpy as jnp

def _softmax(x, axis=-1):
    return jax.nn.softmax(x, axis=axis)

def _gelu(x):
    return jax.nn.gelu(x, approximate=True)

def _silu(x):
    return jax.nn.silu(x)

def _sigmoid(x):
    return jax.nn.sigmoid(x)

def _layernorm(x, axis=-1, eps=1e-05):
    m = jnp.mean(x, axis=axis, keepdims=True)
    v = jnp.var(x, axis=axis, keepdims=True)
    return (x - m) / jnp.sqrt(v + eps)

def _scatter_add(tgt, idx, src, axis=0):
    return tgt.at[idx].add(src)

def _segment_sum(src, seg, n):
    return jax.ops.segment_sum(src, seg, n)
kernel_name = 'mk_recurrent_d1_jaxref_r8_23be85'

def setup_inputs(seed: int=0):
    np.random.seed(seed)
    _w = jnp.asarray

    def _L0_attn_setup():
        import jax, jax.numpy as jnp
        import numpy as np
        import math
        D_MODEL = 512
        N_HEADS = 32
        HEAD_DIM = D_MODEL // N_HEADS
        CLIP_QKV = 8.0
        ALIBI_BIAS_MAX = 8
        LN_EPS = 1e-05

        def _alibi_slopes(total_num_heads: int, alibi_bias_max: int) -> jnp.ndarray:
            next_p2 = 2 ** math.ceil(math.log2(total_num_heads))
            m = jnp.arange(1, next_p2 + 1, dtype=jnp.float32) * (alibi_bias_max / next_p2)
            slopes = 1.0 / jnp.power(2.0, m)
            if next_p2 != total_num_heads:
                slopes = jnp.concatenate([slopes[1::2], slopes[::2]])[:total_num_heads]
            return slopes

        def _layer_norm(x, w, b):
            mu = jnp.mean(x, axis=-1, keepdims=True)
            var = jnp.var(x, axis=-1, keepdims=True)
            return (x - mu) * jax.lax.rsqrt(var + LN_EPS) * w + b
        key = jax.random.key(seed)
        k0, k1, k2 = jax.random.split(key, 3)
        B, S = (2, 256)
        return {'hidden_states': jax.random.normal(k0, (B, S, D_MODEL), dtype=jnp.float32), 'w_qkv': jax.random.normal(k1, (3 * D_MODEL, D_MODEL), dtype=jnp.float32) * 0.02, 'q_ln_w': jnp.ones((D_MODEL,), jnp.float32), 'q_ln_b': jnp.zeros((D_MODEL,), jnp.float32), 'k_ln_w': jnp.ones((D_MODEL,), jnp.float32), 'k_ln_b': jnp.zeros((D_MODEL,), jnp.float32), 'w_out': jax.random.normal(k2, (D_MODEL, D_MODEL), dtype=jnp.float32) * 0.02}
    _L0_attn_in = _L0_attn_setup()

    def _L0_ffn_setup():
        import jax, jax.numpy as jnp
        import numpy as np
        B_, S, D_IN, D_OUT = (4, 256, 512, 512)
        N, RANK, ALPHA = (8, 16, 32)
        SCALE = ALPHA / RANK
        key = jax.random.key(seed)
        kx, ka, kb, kw, kbias = jax.random.split(key, 5)
        x = jax.random.normal(kx, (B_, S, D_IN), dtype=jnp.float32)
        lora_A = jax.random.normal(ka, (N, RANK, D_IN), dtype=jnp.float32) * (1.0 / np.sqrt(D_IN))
        lora_B = jax.random.normal(kb, (N, D_OUT, RANK), dtype=jnp.float32) * (1.0 / np.sqrt(RANK))
        W = jax.random.normal(kw, (D_OUT, D_IN), dtype=jnp.float32) * (1.0 / np.sqrt(D_IN))
        bias = jax.random.normal(kbias, (D_OUT,), dtype=jnp.float32) * 0.01
        lora_weights = jnp.full((N,), 1.0 / N, dtype=jnp.float32)
        return {'x': x, 'lora_A': lora_A, 'lora_B': lora_B, 'W': W, 'bias': bias, 'lora_weights': lora_weights}
    _L0_ffn_in = _L0_ffn_setup()
    _d = {'L0_attn_hidden_states': _L0_attn_in['hidden_states'], 'L0_attn_w_qkv': _L0_attn_in['w_qkv'], 'L0_attn_q_ln_w': _L0_attn_in['q_ln_w'], 'L0_attn_q_ln_b': _L0_attn_in['q_ln_b'], 'L0_attn_k_ln_w': _L0_attn_in['k_ln_w'], 'L0_attn_k_ln_b': _L0_attn_in['k_ln_b'], 'L0_attn_w_out': _L0_attn_in['w_out'], 'L0_ffn_lora_A': _L0_ffn_in['lora_A'], 'L0_ffn_lora_B': _L0_ffn_in['lora_B'], 'L0_ffn_W': _L0_ffn_in['W'], 'L0_ffn_bias': _L0_ffn_in['bias'], 'L0_ffn_lora_weights': _L0_ffn_in['lora_weights']}
    _x0 = _d['L0_attn_hidden_states']
    _d['L0_attn_hidden_states'] = jax.random.normal(jax.random.fold_in(jax.random.key(seed), 1), (2, 1024, 512), dtype=_x0.dtype)
    del _x0
    return _d

def reference(L0_attn_hidden_states, L0_attn_w_qkv, L0_attn_q_ln_w, L0_attn_q_ln_b, L0_attn_k_ln_w, L0_attn_k_ln_b, L0_attn_w_out, L0_ffn_lora_A, L0_ffn_lora_B, L0_ffn_W, L0_ffn_bias, L0_ffn_lora_weights):

    def _L0_attn_ref(hidden_states, w_qkv, q_ln_w, q_ln_b, k_ln_w, k_ln_b, w_out):
        import jax, jax.numpy as jnp
        import numpy as np
        import math
        D_MODEL = 512
        N_HEADS = 32
        HEAD_DIM = D_MODEL // N_HEADS
        CLIP_QKV = 8.0
        ALIBI_BIAS_MAX = 8
        LN_EPS = 1e-05

        def _alibi_slopes(total_num_heads: int, alibi_bias_max: int) -> jnp.ndarray:
            next_p2 = 2 ** math.ceil(math.log2(total_num_heads))
            m = jnp.arange(1, next_p2 + 1, dtype=jnp.float32) * (alibi_bias_max / next_p2)
            slopes = 1.0 / jnp.power(2.0, m)
            if next_p2 != total_num_heads:
                slopes = jnp.concatenate([slopes[1::2], slopes[::2]])[:total_num_heads]
            return slopes

        def _layer_norm(x, w, b):
            mu = jnp.mean(x, axis=-1, keepdims=True)
            var = jnp.var(x, axis=-1, keepdims=True)
            return (x - mu) * jax.lax.rsqrt(var + LN_EPS) * w + b
        B, S, D = hidden_states.shape
        qkv = jnp.einsum('bsd,ed->bse', hidden_states, w_qkv)
        qkv = jnp.clip(qkv, -CLIP_QKV, CLIP_QKV)
        q, k, v = jnp.split(qkv, 3, axis=-1)
        q = _layer_norm(q, q_ln_w, q_ln_b)
        k = _layer_norm(k, k_ln_w, k_ln_b)
        q = q.reshape(B, S, N_HEADS, HEAD_DIM)
        k = k.reshape(B, S, N_HEADS, HEAD_DIM)
        v = v.reshape(B, S, N_HEADS, HEAD_DIM)
        scale = HEAD_DIM ** (-0.5)
        scores = jnp.einsum('bqhd,bkhd->bhqk', q, k) * scale
        pos = jnp.arange(S)
        rel = pos[None, :] - pos[:, None]
        slopes = _alibi_slopes(N_HEADS, ALIBI_BIAS_MAX)
        bias = slopes[:, None, None] * rel.astype(jnp.float32)
        causal = rel <= 0
        scores = jnp.where(causal[None, None], scores + bias[None], -jnp.inf)
        probs = jax.nn.softmax(scores, axis=-1)
        attn = jnp.einsum('bhqk,bkhd->bqhd', probs, v).reshape(B, S, D)
        return jnp.einsum('bsd,ed->bse', attn, w_out)

    def _L0_ffn_ref(x, lora_A, lora_B, W, bias, lora_weights):
        import jax, jax.numpy as jnp
        import numpy as np
        B_, S, D_IN, D_OUT = (4, 256, 512, 512)
        N, RANK, ALPHA = (8, 16, 32)
        SCALE = ALPHA / RANK
        h = jnp.einsum('bsd,nrd->nbsr', x, lora_A)
        coef = (SCALE * lora_weights)[:, None, None]
        lora_out = jnp.einsum('nbsr,nor->bso', h, lora_B * coef)
        base = jnp.einsum('bsd,od->bso', x, W) + bias
        return base + lora_out
    x = L0_attn_hidden_states
    xn = _layernorm(x, axis=-1)
    s = _L0_attn_ref(xn, L0_attn_w_qkv, L0_attn_q_ln_w, L0_attn_q_ln_b, L0_attn_k_ln_w, L0_attn_k_ln_b, L0_attn_w_out)
    g = _silu(_L0_ffn_ref(xn, L0_ffn_lora_A, L0_ffn_lora_B, L0_ffn_W, L0_ffn_bias, L0_ffn_lora_weights))
    x = x + s * g
    return x

_drawn_inputs = setup_inputs


def setup_inputs(seed=0):
    import zlib

    import numpy as np

    out = dict(_drawn_inputs(seed))
    spreads = {'L0_attn_q_ln_w': (1.0, 0.6),
     'L0_attn_q_ln_b': (0.0, 0.8),
     'L0_attn_k_ln_w': (1.0, 0.6),
     'L0_attn_k_ln_b': (0.0, 2.0),
     'L0_ffn_lora_weights': (0.125, 0.6)}
    factors = {'L0_ffn_bias': 64.0}
    for name, (base, spread) in spreads.items():
        noise = np.random.default_rng([zlib.crc32(name.encode()), seed]).standard_normal(out[name].shape)
        drawn = base * np.exp(spread * noise) if base else spread * noise
        out[name] = jnp.asarray(drawn.astype(out[name].dtype))
    for name, factor in factors.items():
        out[name] = (out[name] * factor).astype(out[name].dtype)
    return out
```

```python
from contextlib import ExitStack

import concourse.bass as bass
from concourse import mybir

F32 = mybir.dt.float32
F32R = mybir.dt.float32r
BF16 = mybir.dt.bfloat16
ALU = mybir.AluOpType
ACT = mybir.ActivationFunctionType
AX = mybir.AxisListType

P = 128
B, S, D = 2, 1024, 512
H = 32
HD = D // H
DC = D // P
TILES = B * S // P
GT = 4
GROUPS = TILES // GT
SB = S // P
CLIP = 8.0
LN_EPS = 1e-5
NR, LR = 8, 16
LORA_SCALE = 32 / LR

QH = 4
QUADS = B * H // QH
BUFS = 3
R_ALIBI, R_DOT, R_MAX = 0, 4, 4 + 3 * HD
K_MAX = R_MAX
K_EXP = R_MAX + 2
CW = 512
MASKED = -1e30

UNITS = [(c, kb) for c in range(2) for kb in range(4 * (c + 1))]
NU = len(UNITS)


def unit_cols(c, kb):
    q0 = max(CW * c, P * kb)
    return q0, CW * (c + 1) - q0


def is_diag(c, kb):
    return kb >= 4 * c


def max_pieces():
    out = []
    for qb in range(SB):
        for kc in range(qb // 4 + 1):
            w = min(CW, P * (qb + 1) - CW * kc)
            nh = 2 if w <= CW // 2 else 1
            out += [(qb, kc, h0, nh, w) for h0 in range(0, QH, nh)]
    return out


PIECES = max_pieces()
NP = len(PIECES)
NP0 = sum(p[0] < 4 for p in PIECES)


def piece_schedule():
    ucost = [4 * unit_cols(*u)[1] for u in UNITS]
    pcost = [p[3] * p[4] for p in PIECES]
    total_u, total_p = sum(ucost), sum(pcost)
    done, out, acc, pacc = 0, [], 0, 0
    for u in range(NU):
        acc += ucost[u]
        while done < NP and (pacc + pcost[done]) * total_u <= acc * total_p * 1.02:
            pacc += pcost[done]
            done += 1
        out.append(done)
    out[-1] = NP
    return out


SCHED = piece_schedule()
U_M1 = 1
U_O0 = 6
U_M0 = next(u for u in range(NU) if SCHED[u] >= NP0) + 1


def build(nc, x_in, w_qkv, q_w, q_b, k_w, k_b, w_out, lora_a, lora_b, ffn_w, ffn_bias, lora_w, alibi, out):
    with ExitStack() as ctx:
        sem = lambda name: ctx.enter_context(nc.semaphore(name))
        sb = lambda name, shape, dt: ctx.enter_context(nc.sbuf_tensor(name, shape, dt))
        scratch = {(t, part): nc.dram_tensor(f"{t}_{part}_scratch", [B, D, S], F32, kind="Internal").ap()
                   for t in "qk" for part in ("hi", "lo")}
        alibi_scratch = nc.dram_tensor("alibi_scratch", [2, B * H, 4, S], F32, kind="Internal").ap()

        bank = [ctx.enter_context(nc.psum_tensor(f"bank{i}", [P, 512], F32)) for i in range(4)]
        score_t = ctx.enter_context(nc.psum_tensor("score_t", [P, 4, 512], F32))

        v_all = sb("v_all", [P, QUADS, SB, QH * HD], F32)
        z_all = sb("z_all", [P, TILES, D], F32)
        ident = sb("ident", [P, P], F32)
        ident_b = sb("ident_b", [P, P], BF16)
        mask_b = sb("mask_b", [P, P], BF16)

        project_stage(nc, sem, bank, score_t, scratch, alibi_scratch, v_all, z_all, ident, ident_b, mask_b,
                      x_in, w_qkv, q_w, q_b, k_w, k_b, lora_a, lora_b, ffn_w, ffn_bias, lora_w, alibi)
        attn = sb("attn", [P, QUADS, SB, QH * HD], F32)
        attend_stage(nc, sem, bank, score_t, scratch, alibi_scratch, v_all, ident, ident_b, mask_b, attn)
        combine_stage(nc, sem, bank, x_in, w_out, z_all, attn, ident, out)


def project_stage(nc, sem, bank, score_t, scratch, alibi_scratch, v_all, z_all, ident, ident_b, mask_b,
                  x_in, w_qkv, q_w, q_b, k_w, k_b, lora_a, lora_b, ffn_w, ffn_bias, lora_w, alibi):
    WG = 4
    with ExitStack() as ctx:
        sb = lambda name, shape, dt: ctx.enter_context(nc.sbuf_tensor(name, shape, dt))
        wt_hi = sb("wt_hi", [P, DC, WG * D], F32R)
        wt_lo = sb("wt_lo", [P, DC, WG * D], F32R)
        w_raw = [sb(f"w_raw{i}", [P, 4, D], F32) for i in range(2)]
        xt = sb("xt", [P, GT, D], F32)
        xT_hi = [sb(f"xT_hi{i}", [P, DC, P], F32R) for i in range(2)]
        xT_lo = [sb(f"xT_lo{i}", [P, DC, P], F32R) for i in range(2)]
        qk = sb("qk", [P, 2, GT, D], F32)
        full = [sb(f"full{i}", [P, GT * P], F32) for i in range(2)]
        hi = [sb(f"hi{i}", [P, GT * P], F32R) for i in range(2)]
        lo = [sb(f"lo{i}", [P, GT * P], F32R) for i in range(2)]
        bias_bc = sb("bias_bc", [P, D], F32)
        la = sb("la", [P, D], F32)
        lb = sb("lb", [P, DC, NR * LR], F32)
        lbt = sb("lbt", [P, D], F32)
        lwb = sb("lwb", [P, NR], F32)
        ln_w = sb("ln_w", [P, 2, DC], F32)
        ln_b = sb("ln_b", [P, 2, DC], F32)
        eps = sb("eps", [P, 1], F32)
        alibi_r = sb("alibi_r", [P, 2, S], F32R)
        st = sb("st", [P, 3, 6], F32)
        mv = sb("mv", [P, 3, 2], F32)
        sd = sb("sd", [P, 3], F32)
        rs = sb("rs", [P, 3], F32)

        consts = sem("consts")
        x_in_sem = [sem(f"x_loaded{i}") for i in range(GT)]
        w_in_sem = [sem(f"w_loaded{i}") for i in range(2)]
        small_in = sem("small_loaded")
        alibi_in = sem("alibi_loaded")
        alibi_cut = sem("alibi_cut")
        stored = sem("alibi_stored")
        lb_scaled = sem("lora_b_scaled")
        ln_scaled = sem("ln_scaled")
        lb_turned = sem("lora_b_turned")
        lbt_ready = sem("lora_bt_ready")
        w_turned = sem("w_turned")
        w_hi_done = sem("w_hi_done")
        w_lo_done = sem("w_lo_done")
        x_stat = sem("x_stat")
        x_sd = sem("x_sd")
        x_norm = sem("x_norm")
        x_turned = sem("x_turned")
        x_hi = sem("x_hi")
        x_lo = sem("x_lo")
        q_out = sem("q_out")
        k_out = sem("k_out")
        v_out = sem("v_out")
        z_out = sem("z_out")
        qk_clip = sem("qk_clip")
        v_done = sem("v_done")
        z_done = sem("z_done")
        qk_stat = sem("qk_stat")
        qk_sd = sem("qk_sd")
        qk_norm = sem("qk_norm")
        qk_turned = sem("qk_turned")
        qk_full = sem("qk_full")
        qk_hi = sem("qk_hi")
        qk_lo = sem("qk_lo")
        qk_store = [sem(f"qk_stored{i}") for i in range(2)]
        waited = sem("waited")
        dve = sem("dve_chain")
        turn_bank = [bank[0], bank[1]]
        out_bank = [score_t[:, i, :] for i in range(4)]
        qk_bank = [bank[2], bank[3]]
        xr = x_in.rearrange("b (t p) d -> (b t) p d", p=P)
        w_src = [w_qkv[g * D:(g + 1) * D, :] for g in range(3)] + [ffn_w]
        CHUNKS = 2 * DC
        SMALL = 16 * (1 + DC + 2 + 4 * DC)
        FULL0, LO0, STORE0 = 2, 2, 32
        vt = v_all[:, :, :, :].rearrange("p (b m) k f -> p b m k f", b=B)

        def groups(eng, body):
            with eng.Fori(0, GROUPS - 1) as g:
                body(g, False)
            body(GROUPS - 1, True)

        with nc.Block() as block:
            @block.sync
            def _(sp):
                for t in range(GT):
                    sp.dma_start(xt[:, t, :], xr[t]).then_inc(x_in_sem[t], 16)
                sp.dma_start(w_raw[0][:, :, :], w_src[0].rearrange("(t p) d -> p t d", p=P)).then_inc(w_in_sem[0], 16)
                sp.dma_start(w_raw[1][:, :, :], w_src[1].rearrange("(t p) d -> p t d", p=P)).then_inc(w_in_sem[1], 16)
                sp.dma_start(la[:, :], lora_a.rearrange("n r d -> (n r) d")).then_inc(small_in, 16)
                for t in range(DC):
                    sp.dma_start(lb[:, t, :].rearrange("p (n r) -> p n r", n=NR),
                                 lora_b[:, t * P:(t + 1) * P, :].rearrange("n p r -> p n r")).then_inc(small_in, 16)
                sp.dma_start(lwb[:, :], lora_w.rearrange("(a n) -> a n", a=1).broadcast_to([P, NR])).then_inc(small_in, 16)
                sp.dma_start(bias_bc[:, :], ffn_bias.rearrange("(a n) -> a n", a=1).broadcast_to([P, D])).then_inc(small_in, 16)
                for i, (w, b) in enumerate(((q_w, q_b), (k_w, k_b))):
                    for c in range(DC):
                        sp.dma_start(ln_w[:, i, c:c + 1], w[c * P:(c + 1) * P].rearrange("(p a) -> p a", a=1)).then_inc(small_in, 16)
                        sp.dma_start(ln_b[:, i, c:c + 1], b[c * P:(c + 1) * P].rearrange("(p a) -> p a", a=1)).then_inc(small_in, 16)
                for g in (2, 3):
                    sp.wait_ge(w_turned, DC * (g - 1))
                    sp.dma_start(w_raw[g % 2][:, :, :], w_src[g].rearrange("(t p) d -> p t d", p=P)).then_inc(w_in_sem[g % 2], 16)
                sp.wait_ge(w_turned, DC * 3)
                for i in range(2):
                    if i:
                        sp.wait_ge(alibi_cut, 1)
                    sp.dma_start(w_raw[0][:, 0:2, :].rearrange("p a n -> p (a n)"), alibi[i]).then_inc(alibi_in, 16)
                    sp.wait_ge(alibi_cut, i + 1)
                    for b in range(B):
                        sp.dma_start(alibi_scratch[i, b * H:(b + 1) * H].rearrange("h r s -> (h r) s"),
                                     alibi_r[:, i, :].bitcast(F32)).then_inc(stored, 16)

                def body(g, last):
                    if not last:
                        for t in range(GT):
                            sp.wait_ge(x_turned, g * GT + t + 1)
                            sp.dma_start(xt[:, t, :], xr[bass.ds(g * GT + GT + t, 1)].rearrange("a p d -> (a p) d")).then_inc(x_in_sem[t], 16)
                    for u in range(CHUNKS):
                        name, c = "qk"[u // DC], u % DC
                        for part, src, ready, start in (("hi", hi, qk_hi, 0), ("lo", lo, qk_lo, LO0)):
                            sp.wait_ge(ready, g * CHUNKS + u + 1 + start)
                            half = g >> 1
                            dst = scratch[name, part][bass.ds(half, 1), c * P:(c + 1) * P,
                                                      bass.ds((g % 2) * CW, CW)].rearrange("a p t -> (a p) t")
                            sp.dma_start(dst, src[u % 2][:, :].bitcast(F32)).then_inc(qk_store[u % 2], 16)
                groups(sp, body)
                for i in range(2):
                    sp.wait_ge(qk_store[i], 16 * CHUNKS * GROUPS + STORE0)
                sp.wait_ge(stored, 16 * 2 * B)

            @block.gpsimd
            def _(pool):
                pool.memset(eps[:, :], LN_EPS).then_inc(consts, 1)
                for m, v in ((ident, 0.0), (ident_b, 0.0), (mask_b, 0.0)):
                    pool.memset(m[:, :], v).then_inc(consts, 1)
                pool.wait_ge(consts, 4)
                for m in (ident, ident_b):
                    pool.affine_select(out=m[:, :], in_=m[:, :], compare_op=ALU.not_equal, fill=1.0, base=0,
                                       pattern=[[-1, P]], channel_multiplier=1).then_inc(consts, 1)
                pool.affine_select(out=mask_b[:, :], in_=mask_b[:, :], compare_op=ALU.is_ge, fill=MASKED, base=0,
                                   pattern=[[-1, P]], channel_multiplier=1).then_inc(consts, 1)
                pool.sem_inc(qk_lo, LO0)
                for i in range(2):
                    pool.sem_inc(qk_store[i], STORE0)

                def body(g, last):
                    for u in range(CHUNKS):
                        pool.wait_ge(qk_hi, g * CHUNKS + u + 1)
                        pool.wait_ge(qk_store[u % 2], (g * DC + u // 2) * 32 + STORE0)
                        pool.tensor_tensor(lo[u % 2][:, :], full[u % 2][:, :], hi[u % 2][:, :].bitcast(F32),
                                           ALU.subtract).then_inc(qk_lo, 1)
                groups(pool, body)

            @block.scalar
            def _(act):
                act.sem_inc(qk_full, FULL0)
                for n in range(WG * DC):
                    g, dc = n // DC, n % DC
                    act.wait_ge(w_turned, n + 1)
                    act.activation(wt_hi[:, dc, g * D:(g + 1) * D], qk_bank[n % 2][:, :], ACT.Copy).then_inc(w_hi_done, 1)

                def x_deviation(n):
                    act.wait_ge(x_stat, n + 1)
                    act.activation(sd[:, 2:3], mv[:, 2, 1:2], ACT.Sqrt, bias=eps[:, 0:1]).then_inc(x_sd, 1)

                def x_split(n, par):
                    act.wait_ge(x_turned, n + 1)
                    act.activation(xT_hi[par][:, :, :], turn_bank[par][:, :].rearrange("p (c t) -> p c t", c=DC),
                                   ACT.Copy).then_inc(x_hi, 1)

                act.wait_ge(consts, 7)
                x_deviation(0)
                x_split(0, 0)
                act.wait_ge(small_in, SMALL)
                act.wait_ge(ln_scaled, 1)

                def body(g, last):
                    for t in range(GT):
                        n = g * GT + t
                        nxt = not (last and t == GT - 1)
                        if nxt:
                            x_deviation(n + 1)
                        act.wait_ge(qk_stat, n + 1)
                        act.activation(sd[:, 0:2], mv[:, 0:2, 1], ACT.Sqrt, bias=eps[:, 0:1]).then_inc(qk_sd, 1)
                        if nxt:
                            x_split(n + 1, (t + 1) % 2)
                    for u in range(CHUNKS):
                        i, c = u // DC, u % DC
                        act.wait_ge(qk_turned, g * CHUNKS + u + 1)
                        act.wait_ge(qk_lo, g * CHUNKS + u - 1 + LO0)
                        act.wait_ge(qk_store[u % 2], (g * DC + u // 2) * 32 + STORE0)
                        act.activation(full[u % 2][:, :], qk_bank[u % 2][:, :], ACT.Identity,
                                       bias=ln_b[:, i, c:c + 1], scale=ln_w[:, i, c:c + 1]).then_inc(qk_full, 1)
                        act.wait_ge(qk_full, g * CHUNKS + u + 1 + FULL0)
                        act.activation(hi[u % 2][:, :], full[u % 2][:, :], ACT.Copy).then_inc(qk_hi, 1)
                groups(act, body)

            @block.tensor
            def _(pe):
                pe.wait_ge(consts, 7)

                def turn_weights(n):
                    g, dc = n // DC, n % DC
                    if dc == 0:
                        pe.wait_ge(w_in_sem[g % 2], 16 * (g // 2 + 1))
                    if n >= 2:
                        pe.wait_ge(w_hi_done, n - 1)
                        pe.wait_ge(w_lo_done, n - 1)
                    dst = qk_bank[n % 2]
                    if g < 3:
                        for t in range(4):
                            mm = pe.transpose(dst[:, t * P:(t + 1) * P], w_raw[g % 2][:, t, dc * P:(dc + 1) * P], ident[:, :])
                    else:
                        pe.wait_ge(lbt_ready, 1)
                        pe.matmul(dst[:, :], la[:, dc * P:(dc + 1) * P], lbt[:, :], start=True, stop=False)
                        for t in range(4):
                            mm = pe.matmul(dst[:, t * P:(t + 1) * P], w_raw[g % 2][:, t, dc * P:(dc + 1) * P], ident[:, :],
                                           start=False, stop=(t == 3))
                    mm.then_inc(w_turned, 1)

                def turn_x(n, t):
                    pe.wait_ge(x_norm, n + 1)
                    for c in range(DC):
                        mm = pe.transpose(turn_bank[t % 2][:, c * P:(c + 1) * P], xt[:, t, c * P:(c + 1) * P], ident[:, :])
                    mm.then_inc(x_turned, 1)

                def project(n, t, which, signal):
                    wcols = slice(which * D, (which + 1) * D)
                    terms = [(xT_hi, wt_hi), (xT_hi, wt_lo), (xT_lo, wt_hi)]
                    for j, (a, w) in enumerate(terms):
                        for c in range(DC):
                            mm = pe.matmul(out_bank[which], a[t % 2][:, c, :], w[:, c, wcols],
                                           start=(j == 0 and c == 0), stop=(j == 2 and c == DC - 1))
                    mm.then_inc(signal, 1)

                pe.wait_ge(lb_scaled, 1)
                for t in range(DC):
                    mm = pe.transpose(turn_bank[1][:, t * P:(t + 1) * P], lb[:, t, :], ident[:, :])
                mm.then_inc(lb_turned, 1)
                for n in range(WG * DC):
                    turn_weights(n)
                pe.wait_ge(lbt_ready, 1)
                turn_x(0, 0)
                pe.wait_ge(w_hi_done, WG * DC)
                pe.wait_ge(w_lo_done, WG * DC)

                def body(g, last):
                    for t in range(GT):
                        n = g * GT + t
                        pe.wait_ge(x_hi, n + 1)
                        pe.wait_ge(x_lo, n + 1)
                        pe.wait_ge(qk_clip, 2 * n + 1)
                        project(n, t, 0, q_out)
                        pe.wait_ge(qk_clip, 2 * n + 2)
                        project(n, t, 1, k_out)
                        pe.wait_ge(v_done, n + 1)
                        project(n, t, 2, v_out)
                        if not (last and t == GT - 1):
                            turn_x(n + 1, (t + 1) % GT)
                        pe.wait_ge(z_done, n + 1)
                        project(n, t, 3, z_out)
                    for u in range(CHUNKS):
                        i, c = u // DC, u % DC
                        pe.wait_ge(qk_norm, (g + 1) * GT)
                        pe.wait_ge(qk_full, g * CHUNKS + u - 1 + FULL0)
                        for t in range(GT):
                            mm = pe.transpose(qk_bank[u % 2][:, t * P:(t + 1) * P], qk[:, i, t, c * P:(c + 1) * P], ident[:, :])
                        mm.then_inc(qk_turned, 1)
                groups(pe, body)

            @block.vector
            def _(v):
                v.sem_inc(qk_clip, 2)
                v.sem_inc(v_done, 1)
                v.sem_inc(z_done, 1)
                v.wait_ge(small_in, SMALL)
                for t in range(DC):
                    lbv = lb[:, t, :].rearrange("p (n r) -> p n r", n=NR)
                    ins = v.tensor_tensor(lbv, lbv, lwb[:, :].unsqueeze(2).broadcast_to([P, NR, LR]), ALU.mult)
                ins.then_inc(lb_scaled, 1)
                for par in (ln_w, ln_b):
                    ins = v.tensor_scalar(par[:, 0, :], par[:, 0, :], HD ** -0.5, None, ALU.mult)
                ins.then_inc(ln_scaled, 1)
                v.wait_ge(lb_turned, 1)
                v.tensor_scalar(lbt[:, :], turn_bank[1][:, :], LORA_SCALE, None, ALU.mult).then_inc(lbt_ready, 1)
                for n in range(WG * DC):
                    g, dc = n // DC, n % DC
                    v.wait_ge(w_hi_done, n + 1)
                    v.tensor_tensor(wt_lo[:, dc, g * D:(g + 1) * D], qk_bank[n % 2][:, :],
                                    wt_hi[:, dc, g * D:(g + 1) * D].bitcast(F32), ALU.subtract).then_inc(w_lo_done, 1)

                CHAIN = 5
                chained = [0]

                def chain(ins, base):
                    chained[0] += 1
                    ins.then_inc(dve, 1)
                    v.wait_ge(dve, base + chained[0])

                def stats(slot, src, base):
                    chain(v.bn_stats(st[:, slot, :], src), base)
                    v.sem_inc(waited, 1)
                    return v.bn_aggr(mv[:, slot, :], st[:, slot, :])

                def x_stats(t, k, base):
                    v.wait_ge(x_in_sem[t], 16 * k)
                    stats(2, xt[:, t, :], base).then_inc(x_stat, 1)

                def x_normalise(n, t, base):
                    v.wait_ge(x_sd, n + 1)
                    chain(v.reciprocal(rs[:, 2:3], sd[:, 2:3]), base)
                    v.tensor_scalar(xt[:, t, :], xt[:, t, :], mv[:, 2, 0:1], rs[:, 2:3], ALU.subtract, ALU.mult).then_inc(x_norm, 1)

                def x_split(n, par):
                    v.wait_ge(x_hi, n + 1)
                    v.tensor_tensor(xT_lo[par][:, :, :], turn_bank[par][:, :].rearrange("p (c t) -> p c t", c=DC),
                                    xT_hi[par][:, :, :].bitcast(F32), ALU.subtract).then_inc(x_lo, 1)

                x_stats(0, 1, 0)
                x_normalise(0, 0, 0)
                x_split(0, 0)
                for i in range(2):
                    v.wait_ge(alibi_in, 16 * (i + 1))
                    v.tensor_copy(alibi_r[:, i, :], w_raw[0][:, 0:2, :].rearrange("p a n -> p (a n)")).then_inc(alibi_cut, 1)
                first = chained[0]

                def body(g, last):
                    for t in range(GT):
                        n = g * GT + t
                        nxt = not (last and t == GT - 1)
                        base = n * CHAIN + first
                        chained[0] = 0
                        if nxt:
                            x_stats((t + 1) % GT, g + 1 + (t + 1) // GT, base)
                        for i, ready in ((0, q_out), (1, k_out)):
                            v.wait_ge(ready, n + 1)
                            v.tensor_scalar(qk[:, i, t, :], out_bank[i], -CLIP, CLIP, ALU.max, ALU.min).then_inc(qk_clip, 1)
                            v.wait_ge(qk_clip, 2 * n + i + 3)
                            agg = stats(i, qk[:, i, t, :], base)
                        agg.then_inc(qk_stat, 1)
                        if nxt:
                            x_normalise(n + 1, (t + 1) % GT, base)
                        v.wait_ge(v_out, n + 1)
                        half = g >> 1
                        dst = vt[:, bass.ds(half, 1), :, bass.ds((g % 2) * GT + t, 1), :].rearrange("p a m k f -> p (a m k) f")
                        v.tensor_scalar(dst, out_bank[2].rearrange("p (m f) -> p m f", f=QH * HD), -CLIP, CLIP,
                                        ALU.max, ALU.min).then_inc(v_done, 1)
                        if nxt:
                            x_split(n + 1, (t + 1) % 2)
                        v.wait_ge(qk_sd, n + 1)
                        chain(v.reciprocal(rs[:, 0:2], sd[:, 0:2]), base)
                        for i in range(2):
                            ins = v.tensor_scalar(qk[:, i, t, :], qk[:, i, t, :], mv[:, i, 0:1], rs[:, i:i + 1],
                                                  ALU.subtract, ALU.mult)
                        ins.then_inc(qk_norm, 1)
                        v.wait_ge(z_out, n + 1)
                        v.tensor_tensor(z_all[:, bass.ds(n, 1), :].rearrange("p a d -> p (a d)"), out_bank[3], bias_bc[:, :],
                                        ALU.add).then_inc(z_done, 1)
                groups(v, body)


def attend_stage(nc, sem, bank, score_t, scratch, alibi_scratch, v_all, ident, ident_b, mask_b, attn):
    with ExitStack() as ctx:
        sb = lambda name, shape, dt: ctx.enter_context(nc.sbuf_tensor(name, shape, dt))
        qT = [sb(f"qT{i}", [P, 2, S], F32R) for i in range(BUFS)]
        kT = [sb(f"kT{i}", [P, 2, S], F32R) for i in range(BUFS)]
        vq = [sb(f"vq{i}", [P, SB, QH, 32], F32) for i in range(BUFS)]
        prob = [sb(f"prob{i}", [P, QH, CW], F32) for i in range(3)]
        oT = [sb(f"oT{i}", [P, CW], F32) for i in range(2)]
        top = sb("top", [P, 2, SB, QH], F32)
        msplit = [sb(f"msplit{i}", [P, 4, QH, 2], F32R) for i in range(2)]
        mrow = [sb(f"mrow{i}", [2 * QH, CW], F32R) for i in range(2)]
        inv = sb("inv", [P, 4, QH], F32)
        ones = sb("ones", [2, CW], F32)
        ones_r = sb("ones_r", [2, CW], F32R)

        score_q = [bank[0], bank[1]]
        out_t = bank[2]
        turn = bank[3]

        loaded = [sem(f"qk_loaded{i}") for i in range(BUFS)]
        ones_set = sem("ones_set")
        ones_in = sem("ones_in")
        quad_free = sem("quad_free")
        v_copied = sem("v_copied")
        piece_out = sem("piece_out")
        piece_max = sem("piece_max")
        top_done = sem("top_done")
        m_split = [sem(f"m_split{c}") for c in range(2)]
        m_hi = [sem(f"m_hi{c}") for c in range(2)]
        v_filled = sem("v_filled")
        turned = sem("turned")
        turn_free = sem("turn_free")
        m_rows = [sem(f"m_rows{c}") for c in range(2)]
        m_in = [sem(f"m_in{c}") for c in range(2)]
        st_out = sem("st_out")
        exp_done = sem("exp_done")
        pv_done = sem("pv_done")
        o_taken = sem("o_taken")
        inv_done = sem("inv_done")
        o_norm = sem("o_norm")
        HU = 2 * NU
        LOADS = 16 * 16
        EXP0, PIECE0, PV0, FREE0, ROWS0, TURN0 = 2, 2, 3, 2, 64, 1
        TAIL = 2

        def quads(eng, step):
            with eng.Fori(0, QUADS // BUFS - 1) as i:
                for s in range(BUFS):
                    step(i * BUFS + s, s, i, BUFS)
            for n in range(QUADS - QUADS % BUFS - BUFS, QUADS):
                step(n, n % BUFS, n // BUFS, QUADS - 1 - n)

        with nc.Block() as block:
            @block.sync
            def _(sp):
                def load(n, s):
                    for tile, t, r in ((kT[s], 1, ("hi", "lo", "hi")), (qT[s], 0, ("hi", "hi", "lo"))):
                        for a in range(2):
                            rows = 64 * a
                            sp.dma_start(tile[rows:rows + 4, :, :].bitcast(F32),
                                         alibi_scratch[t].rearrange("(n j a) r s -> n a r j s", j=2, a=2)[bass.ds(n, 1), a]
                                         .rearrange("x r j s -> (x r) j s")).then_inc(loaded[s], 16)
                            for k, part in enumerate(r):
                                src = scratch["qk"[t], part].rearrange("b (m j a d) s -> (b m) a d j s", j=2, a=2, d=HD)
                                r0 = rows + R_DOT + HD * k
                                sp.dma_start(tile[r0:r0 + HD, :, :].bitcast(F32),
                                             src[bass.ds(n, 1), a].rearrange("x d j s -> (x d) j s")).then_inc(loaded[s], 16)

                def send_rows(s, c):
                    for a in range(2):
                        for j in range(2):
                            y = 2 * a + j
                            r0 = 64 * a + R_MAX
                            sp.dma_start(qT[s][r0:r0 + 2, j, c * CW:(c + 1) * CW].bitcast(F32),
                                         mrow[c][2 * y:2 * y + 2, :].bitcast(F32))\
                              .then_inc(m_in[c], 16)

                load(0, 0)
                sp.wait_ge(ones_set, 2)
                for s in range(BUFS):
                    for a in range(2):
                        for j in range(2):
                            for c in range(2):
                                sp.dma_start(kT[s][64 * a + R_MAX:64 * a + R_MAX + 2, j, c * CW:(c + 1) * CW].bitcast(F32),
                                             ones_r[:, :].bitcast(F32)).then_inc(ones_in, 16)
                load(1, 1)
                sp.wait_ge(m_rows[0], 1)
                send_rows(0, 0)

                def step(n, s, i, left):
                    sp.wait_ge(m_rows[1], n + 1)
                    send_rows(s, 1)
                    if left >= 2:
                        sp.wait_ge(quad_free, n + FREE0)
                        load(n + 2, (s + 2) % BUFS)
                    if left >= 1:
                        sp.wait_ge(m_rows[0], n + 2)
                        send_rows((s + 1) % BUFS, 0)
                quads(sp, step)
                sp.wait_ge(m_in[0], 64 * QUADS)
                sp.wait_ge(m_in[1], 64 * QUADS + ROWS0)

            @block.gpsimd
            def _(pool):
                pool.sem_inc(m_in[1], ROWS0)
                pool.memset(ones[:, :], 1.0).then_inc(ones_set, 1)
                pool.wait_ge(ones_set, 1)
                pool.tensor_copy(ones_r[:, :], ones[:, :]).then_inc(ones_set, 1)
                for i in range(BUFS):
                    pool.memset(vq[i][:, :, :, :], 1.0).then_inc(v_filled, 1)
                pool.wait_ge(v_filled, BUFS)

                def copy_v(n, s):
                    pool.tensor_copy(vq[s][:, :, :, 0:HD], v_all[:, bass.ds(n, 1), :, :]
                                     .rearrange("p a k (h d) -> p (a k) h d", h=QH)).then_inc(v_copied, 1)

                copy_v(0, 0)

                def step(n, s, i, left):
                    if left:
                        pool.wait_ge(quad_free, n - 1 + FREE0)
                        copy_v(n + 1, (s + 1) % BUFS)
                quads(pool, step)

            @block.scalar
            def _(act):
                act.sem_inc(exp_done, EXP0)

                def maxima_rows(c, wait_rows, use):
                    act.wait_ge(turned, use)
                    if wait_rows is not None:
                        act.wait_ge(m_in[c], wait_rows)
                    act.activation(mrow[c][:, :], turn[0:2 * QH, :], ACT.Copy).then_inc(m_rows[c], 1)

                maxima_rows(0, None, 1)

                def take_output(n, c):
                    last_unit = 4 * (c + 1) - 1 if c == 0 else NU - 1
                    act.wait_ge(pv_done, n * NU + last_unit + 1 + PV0)
                    act.activation(oT[c][:, :], out_t[:, :], ACT.Copy).then_inc(o_taken, 1)

                def step(n, s, i, left):
                    for u, (c, kb) in enumerate(UNITS):
                        _, w = unit_cols(c, kb)
                        for j in range(2):
                            act.wait_ge(st_out, n * HU + 2 * u + j + 1)
                            if j == 0:
                                act.wait_ge(pv_done, n * NU + u - 2 + PV0)
                            act.activation(prob[u % 3][:, 2 * j:2 * j + 2, 0:w], score_t[:, 2 * j:2 * j + 2, 0:w],
                                           ACT.Exp).then_inc(exp_done, 1)
                        if u == U_M1:
                            maxima_rows(1, n * 64 + ROWS0, n * 4 + 2)
                        if u == U_M0 and left:
                            maxima_rows(0, n * 64 + 64, n * 4 + 3)
                        if u == 4:
                            take_output(n, 0)
                    take_output(n, 1)
                quads(act, step)

            @block.tensor
            def _(pe):
                pe.sem_inc(pv_done, PV0)
                pe.sem_inc(quad_free, FREE0)

                def piece(q, s, p):
                    qb, kc, h0, nh, w = PIECES[p]
                    pe.wait_ge(piece_max, q * NP + p - 1 + PIECE0)
                    dst = score_q[p % 2]
                    for x in range(nh):
                        a, j = (h0 + x) // 2, (h0 + x) % 2
                        rows = slice(64 * a, 64 * a + K_MAX)
                        mm = pe.matmul(dst[:, x * w:(x + 1) * w], qT[s][rows, j, qb * P:(qb + 1) * P],
                                       kT[s][rows, j, kc * CW:kc * CW + w], start=True, stop=(kc != qb // 4))
                        if kc == qb // 4:
                            mm = pe.matmul(dst[:, (x + 1) * w - P:(x + 1) * w], ident_b[:, :], mask_b[:, :],
                                           start=False, stop=True)
                    mm.then_inc(piece_out, 1)

                def turn_maxima(c, q):
                    pe.wait_ge(m_split[c], q + 1)
                    for b in range(4):
                        mm = pe.transpose(turn[0:2 * QH, b * P:(b + 1) * P],
                                          msplit[c][:, b, :, :].rearrange("p h x -> p (h x)").bitcast(F32), ident[:, :])
                    mm.then_inc(turned, 1)

                def turn_output(n, c):
                    pe.wait_ge(o_taken, 2 * n + c + 1)
                    for b in range(4):
                        mm = pe.transpose(turn[:, b * P:(b + 1) * P], oT[c][:, b * P:(b + 1) * P], ident[:, :])
                        if c == 1 and b == 0:
                            mm.then_inc(quad_free, 1)
                    mm.then_inc(turned, 1)

                def exponents(n, s, u, j):
                    c, kb = UNITS[u]
                    q0, w = unit_cols(c, kb)
                    pe.wait_ge(exp_done, n * HU + 2 * u + j - 1 + EXP0)
                    for a in range(2):
                        rows = slice(64 * a, 64 * a + K_EXP)
                        mm = pe.matmul(score_t[:, 2 * j + a, 0:w], kT[s][rows, j, kb * P:(kb + 1) * P],
                                       qT[s][rows, j, q0:q0 + w], start=True, stop=not is_diag(c, kb))
                    if is_diag(c, kb):
                        for a in range(2):
                            mm = pe.matmul(score_t[:, 2 * j + a, 0:P], mask_b[:, :], ident_b[:, :], start=False, stop=True)
                    mm.then_inc(st_out, 1)

                def apply_v(n, s, u):
                    c, kb = UNITS[u]
                    q0, w = unit_cols(c, kb)
                    pe.wait_ge(exp_done, n * HU + 2 * u + 2 + EXP0)
                    for h in range(QH):
                        mm = pe.matmul(out_t[32 * h:32 * h + 32, q0 - CW * c:q0 - CW * c + w], vq[s][:, kb, h, :],
                                       prob[u % 3][:, h, 0:w], start=(kb == 0), stop=(kb == 4 * (c + 1) - 1))
                    mm.then_inc(pv_done, 1)

                pe.wait_ge(loaded[0], LOADS)
                for p in range(NP):
                    piece(0, 0, p)
                turn_maxima(0, 0)
                pe.wait_ge(ones_in, 16 * 4 * 2 * BUFS)

                def step(n, s, i, left):
                    done = 0
                    pe.wait_ge(m_in[0], n * 64 + 64)
                    pe.wait_ge(v_copied, n + 1)
                    for u in range(NU):
                        if UNITS[u] == (1, 0):
                            pe.wait_ge(m_in[1], n * 64 + 64 + ROWS0)
                        for j in range(2):
                            exponents(n, s, u, j)
                        if left:
                            if u == 0:
                                nxt = (s + 1) % BUFS
                                pe.wait_ge(loaded[nxt], (i + 1 + (s + 1) // BUFS) * LOADS)
                            while done < SCHED[u] - (TAIL if u == NU - 1 else 0):
                                piece(n + 1, nxt, done)
                                done += 1
                        if u == U_M1:
                            pe.wait_ge(m_rows[0], n + 1)
                            pe.wait_ge(turn_free, n * 2 + TURN0)
                            turn_maxima(1, n)
                        if u == U_M0 and left:
                            pe.wait_ge(m_rows[1], n + 1)
                            turn_maxima(0, n + 1)
                        if u >= 1:
                            if u == 5:
                                pe.wait_ge(o_taken, 2 * n + 1)
                            apply_v(n, s, u - 1)
                        if u == U_O0:
                            if left:
                                pe.wait_ge(m_rows[0], n + 2)
                            else:
                                pe.wait_ge(m_rows[1], n + 1)
                            turn_output(n, 0)
                    apply_v(n, s, NU - 1)
                    mm = None
                    if left:
                        while done < NP:
                            piece(n + 1, nxt, done)
                            done += 1
                    pe.wait_ge(turn_free, n * 2 + 1 + TURN0)
                    turn_output(n, 1)
                quads(pe, step)

            @block.vector
            def _(v):
                v.sem_inc(piece_max, PIECE0)
                v.sem_inc(turn_free, TURN0)

                def maxima(q, p):
                    qb, kc, h0, nh, w = PIECES[p]
                    v.wait_ge(piece_out, q * NP + p + 1)
                    v.tensor_reduce(top[:, kc, qb, h0:h0 + nh], score_q[p % 2][:, 0:nh * w].rearrange("p (h w) -> p h w", w=w),
                                    AX.X, ALU.max).then_inc(piece_max, 1)

                def split(q, c, pieces):
                    v.wait_ge(piece_max, q * NP + pieces + PIECE0)
                    if c == 1:
                        v.tensor_tensor(top[:, 0, 4:8, :], top[:, 0, 4:8, :], top[:, 1, 4:8, :], ALU.max).then_inc(top_done, 1)
                        v.wait_ge(top_done, q + 1)
                    m = top[:, 0, 4 * c:4 * c + 4, :]
                    v.tensor_scalar(msplit[c][:, :, :, 0], m, -1.0, None, ALU.mult).then_inc(m_hi[c], 1)
                    v.wait_ge(m_hi[c], q + 1)
                    v.scalar_tensor_tensor(out=msplit[c][:, :, :, 1], in0=m, scalar=-1.0, in1=msplit[c][:, :, :, 0].bitcast(F32),
                                           op0=ALU.mult, op1=ALU.subtract).then_inc(m_split[c], 1)

                def normalise(n, c, use):
                    v.wait_ge(turned, use)
                    o = turn[:, :].rearrange("p (b h x) -> p b h x", b=4, h=QH)
                    v.reciprocal(inv[:, :, :], o[:, :, :, HD]).then_inc(inv_done, 1)
                    v.wait_ge(inv_done, 2 * n + c + 1)
                    dst = attn[:, bass.ds(n, 1), 4 * c:4 * c + 4, :].rearrange("p a b (h d) -> p (a b) h d", h=QH)
                    v.tensor_tensor(dst, o[:, :, :, 0:HD], inv[:, :, :].unsqueeze(3).broadcast_to([P, 4, QH, HD]),
                                    ALU.mult).then_inc(turn_free, 1)

                for p in range(NP):
                    maxima(0, p)
                    if p == NP0 - 1:
                        split(0, 0, NP0)
                split(0, 1, NP)

                def step(n, s, i, left):
                    done = 0
                    for u in range(NU):
                        if left:
                            while done < SCHED[u] - (TAIL if u == NU - 1 else 0):
                                maxima(n + 1, done)
                                done += 1
                                if done == NP0:
                                    split(n + 1, 0, NP0)
                        if u == U_O0:
                            normalise(n, 0, n * 4 + (4 if left else 3))
                    if left:
                        while done < NP:
                            maxima(n + 1, done)
                            done += 1
                        split(n + 1, 1, NP)
                    normalise(n, 1, n * 4 + (5 if left else 4))
                quads(v, step)


def combine_stage(nc, sem, bank, x_in, w_out, z_all, attn, ident, out):
    with ExitStack() as ctx:
        sb = lambda name, shape, dt: ctx.enter_context(nc.sbuf_tensor(name, shape, dt))
        wo_raw = sb("wo_raw", [P, 4, D], F32)
        wo_hi = sb("wo_hi", [P, DC, D], F32R)
        wo_lo = sb("wo_lo", [P, DC, D], F32R)
        at = [sb(f"at{i}", [P, D], F32) for i in range(2)]
        aT_hi = [sb(f"aT_hi{i}", [P, DC, P], F32R) for i in range(2)]
        aT_lo = [sb(f"aT_lo{i}", [P, DC, P], F32R) for i in range(2)]
        xc = [sb(f"xc{i}", [P, D], F32) for i in range(2)]
        gate = [sb(f"gate{i}", [P, D], F32) for i in range(2)]
        prod = [sb(f"prod{i}", [P, D], F32) for i in range(2)]
        y = [sb(f"y{i}", [P, D], F32) for i in range(2)]
        turn_bank, out_bank = [bank[0], bank[1]], [bank[2], bank[3]]

        wo_in = sem("wo_in")
        wo_turned = sem("wo_turned")
        wo_hi_done = sem("wo_hi_done")
        wo_lo_done = sem("wo_lo_done")
        x_loaded = [sem(f"xc_loaded{i}") for i in range(2)]
        staged = sem("staged")
        a_turned = sem("a_turned")
        a_hi = sem("a_hi")
        a_lo = sem("a_lo")
        projected = sem("projected")
        gated = sem("gated")
        multiplied = sem("multiplied")
        y_done = sem("y_done")
        y_stored = [sem(f"y_stored{i}") for i in range(2)]
        xr = x_in.rearrange("b (t p) d -> (b t) p d", p=P)
        yr = out.rearrange("b (t p) d -> (b t) p d", p=P)
        av = attn[:, :, :, :].rearrange("p (b m) k f -> p b m k f", b=B)
        TB = 4
        A0, Y0, MUL0 = 1, 2, 2

        def tiles(eng, step):
            with eng.Fori(0, TILES // TB - 1) as i:
                for t in range(TB):
                    step(i * TB + t, i, t, TB)
            i = TILES // TB - 1
            for t in range(TB):
                step(i * TB + t, i, t, TB - 1 - t)

        with nc.Block() as block:
            @block.sync
            def _(sp):
                sp.dma_start(wo_raw[:, :, :], w_out.rearrange("(t p) d -> p t d", p=P)).then_inc(wo_in, 16)
                for t in range(2):
                    sp.dma_start(xc[t][:, :], xr[t]).then_inc(x_loaded[t], 16)

                def step(n, i, t, left):
                    sp.wait_ge(y_done, n + 1 + Y0)
                    sp.dma_start(yr[bass.ds(n, 1)].rearrange("a p d -> (a p) d"), y[t % 2][:, :]).then_inc(y_stored[t % 2], 16)
                    if left >= 2:
                        sp.dma_start(xc[t % 2][:, :], xr[bass.ds(n + 2, 1)].rearrange("a p d -> (a p) d")).then_inc(x_loaded[t % 2], 16)
                tiles(sp, step)
                for t in range(2):
                    sp.wait_ge(y_stored[t], 16 * TILES // 2 + 16)

            @block.gpsimd
            def _(pool):
                pool.sem_inc(y_done, Y0)
                for t in range(2):
                    pool.sem_inc(y_stored[t], 16)

                def stage(n, i, t):
                    half = (i >> 1) % B
                    pool.tensor_copy(at[t % 2][:, :].rearrange("p (m f) -> p m f", f=QH * HD),
                                     av[:, bass.ds(half, 1), :, bass.ds((i % 2) * TB + t, 1), :]
                                     .rearrange("p a m k f -> p (a m k) f")).then_inc(staged, 1)

                stage(0, 0, 0)

                def step(n, i, t, left):
                    if left:
                        pool.wait_ge(a_turned, n + A0)
                        stage(n + 1, i + (t + 1) // TB, (t + 1) % TB)
                    pool.wait_ge(multiplied, n + 1 + MUL0)
                    pool.wait_ge(x_loaded[t % 2], (i * 2 + t // 2) * 16 + 16)
                    pool.wait_ge(y_stored[t % 2], (i * 2 + t // 2) * 16 + 16)
                    pool.tensor_tensor(y[t % 2][:, :], prod[t % 2][:, :], xc[t % 2][:, :], ALU.add).then_inc(y_done, 1)
                tiles(pool, step)

            @block.scalar
            def _(act):
                for dc in range(DC):
                    act.wait_ge(wo_turned, dc + 1)
                    act.activation(wo_hi[:, dc, :], out_bank[dc % 2][:, :], ACT.Copy).then_inc(wo_hi_done, 1)

                def cut(n, t):
                    act.wait_ge(a_turned, n + 1 + A0)
                    act.activation(aT_hi[t % 2][:, :, :], turn_bank[t % 2][:, :].rearrange("p (c t) -> p c t", c=DC),
                                   ACT.Copy).then_inc(a_hi, 1)

                cut(0, 0)

                def step(n, i, t, left):
                    act.wait_ge(y_done, n - 1 + Y0)
                    act.activation(gate[t % 2][:, :], z_all[:, bass.ds(n, 1), :].rearrange("p a d -> p (a d)"),
                                   ACT.Silu).then_inc(gated, 1)
                    if left:
                        cut(n + 1, t + 1)
                tiles(act, step)

            @block.tensor
            def _(pe):
                pe.wait_ge(wo_in, 16)
                pe.sem_inc(a_turned, A0)
                for dc in range(DC):
                    if dc >= 2:
                        pe.wait_ge(wo_hi_done, dc - 1)
                        pe.wait_ge(wo_lo_done, dc - 1)
                    for t in range(4):
                        mm = pe.transpose(out_bank[dc % 2][:, t * P:(t + 1) * P], wo_raw[:, t, dc * P:(dc + 1) * P], ident[:, :])
                    mm.then_inc(wo_turned, 1)

                def turn_tile(n, t):
                    pe.wait_ge(staged, n + 1)
                    for c in range(DC):
                        mm = pe.transpose(turn_bank[t % 2][:, c * P:(c + 1) * P], at[t % 2][:, c * P:(c + 1) * P], ident[:, :])
                    mm.then_inc(a_turned, 1)

                turn_tile(0, 0)
                pe.wait_ge(wo_hi_done, DC)
                pe.wait_ge(wo_lo_done, DC)

                def step(n, i, t, left):
                    if left:
                        turn_tile(n + 1, t + 1)
                    pe.wait_ge(a_hi, n + 1)
                    pe.wait_ge(a_lo, n + 1)
                    pe.wait_ge(multiplied, n - 1 + MUL0)
                    for j, (a, w) in enumerate([(aT_hi, wo_hi), (aT_hi, wo_lo), (aT_lo, wo_hi)]):
                        for c in range(DC):
                            mm = pe.matmul(out_bank[t % 2][:, :], a[t % 2][:, c, :], w[:, c, :],
                                           start=(j == 0 and c == 0), stop=(j == 2 and c == DC - 1))
                    mm.then_inc(projected, 1)
                tiles(pe, step)

            @block.vector
            def _(v):
                v.sem_inc(multiplied, MUL0)
                for dc in range(DC):
                    v.wait_ge(wo_hi_done, dc + 1)
                    v.tensor_tensor(wo_lo[:, dc, :], out_bank[dc % 2][:, :], wo_hi[:, dc, :].bitcast(F32), ALU.subtract)\
                     .then_inc(wo_lo_done, 1)

                def cut(n, t):
                    v.wait_ge(a_hi, n + 1)
                    v.tensor_tensor(aT_lo[t % 2][:, :, :], turn_bank[t % 2][:, :].rearrange("p (c t) -> p c t", c=DC),
                                    aT_hi[t % 2][:, :, :].bitcast(F32), ALU.subtract).then_inc(a_lo, 1)

                cut(0, 0)

                def step(n, i, t, left):
                    if left:
                        cut(n + 1, t + 1)
                    v.wait_ge(projected, n + 1)
                    v.wait_ge(gated, n + 1)
                    v.wait_ge(y_done, n - 1 + Y0)
                    v.tensor_tensor(prod[t % 2][:, :], out_bank[t % 2][:, :], gate[t % 2][:, :], ALU.mult).then_inc(multiplied, 1)
                tiles(v, step)


_INS = ['L0_attn_hidden_states', 'L0_attn_w_qkv', 'L0_attn_q_ln_w', 'L0_attn_q_ln_b', 'L0_attn_k_ln_w', 'L0_attn_k_ln_b',
        'L0_attn_w_out', 'L0_ffn_lora_A', 'L0_ffn_lora_B', 'L0_ffn_W', 'L0_ffn_bias', 'L0_ffn_lora_weights']


def alibi_rows():
    import numpy as _np
    slopes = (_np.float32(1.0) / _np.power(_np.float32(2.0), _np.arange(1, H + 1, dtype=_np.float32) * _np.float32(8 / H)))
    mant, expo = _np.frexp(slopes)
    s_hi = _np.ldexp(_np.rint(_np.ldexp(mant, 12)), expo - 12).astype(_np.float32)
    s_lo = (slopes - s_hi).astype(_np.float32)
    pos = _np.arange(S, dtype=_np.float32)
    one = _np.ones(S, _np.float32)
    rows = _np.empty((2, H, 4, S), _np.float32)
    for h in range(H):
        rows[0, h] = [s_hi[h] * one, -pos, s_lo[h] * one, -pos]
        rows[1, h] = [pos, s_hi[h] * one, pos, s_lo[h] * one]
    return rows.reshape(2, H * 4, S)


def kernel(**inputs):
    import numpy as _np
    import concourse.bacc as _bacc
    from concourse import mybir as _mybir
    from concourse.bass_utils import run_bass_kernel_spmd as _run

    nc = _bacc.Bacc("TRN2", target_bir_lowering=False, num_devices=1)
    arrays, args = {}, []
    for name in _INS:
        a = _np.ascontiguousarray(inputs[name])
        arrays[f"in_{name}_dram"] = a
        args.append(nc.dram_tensor(f"in_{name}_dram", a.shape, _mybir.dt.from_np(a.dtype), kind="ExternalInput").ap())
    rows = alibi_rows()
    arrays["alibi_dram"] = rows
    args.append(nc.dram_tensor("alibi_dram", rows.shape, _mybir.dt.float32, kind="ExternalInput").ap())
    args.append(nc.dram_tensor("out_0_dram", (B, S, D), _mybir.dt.float32, kind="ExternalOutput").ap())
    build(nc, *args)
    r = _run(nc, [arrays], core_ids=[0])
    return r.results[0]["out_0_dram"]
```

```python
from contextlib import ExitStack

import concourse.bass as bass
from concourse import mybir

F32 = mybir.dt.float32
F32R = mybir.dt.float32r
BF16 = mybir.dt.bfloat16
ALU = mybir.AluOpType
ACT = mybir.ActivationFunctionType
AX = mybir.AxisListType

P = 128
B, S, D = 2, 1024, 512
H = 32
HD = D // H
DC = D // P
TILES = B * S // P
GT = 4
GROUPS = TILES // GT
SB = S // P
CLIP = 8.0
LN_EPS = 1e-5
NR, LR = 8, 16
LORA_SCALE = 32 / LR

QH = 4
QUADS = B * H // QH
BUFS = 3
PARTS = 3
N_ALIBI = 4 * PARTS
TERMS = [(0, 0), (0, 1), (0, 2), (1, 0), (1, 1), (2, 0)]
R_DOT = N_ALIBI
R_MAX = R_DOT + len(TERMS) * HD
K_MAX = R_MAX
K_EXP = R_MAX + PARTS
CW = 512
MASKED = -1e30

UNITS = [(c, kb) for c in range(2) for kb in range(4 * (c + 1))]
NU = len(UNITS)


def unit_cols(c, kb):
    q0 = max(CW * c, P * kb)
    return q0, CW * (c + 1) - q0


def is_diag(c, kb):
    return kb >= 4 * c


def max_pieces():
    out = []
    for qb in range(SB):
        for kc in range(qb // 4 + 1):
            w = min(CW, P * (qb + 1) - CW * kc)
            nh = {128: 4, 256: 2}.get(w, 1)
            out += [(qb, kc, h0, nh, w) for h0 in range(0, QH, nh)]
    return out


PIECES = max_pieces()
NP = len(PIECES)
NP0 = sum(p[0] < 4 for p in PIECES)


def piece_schedule():
    cost = []
    for u in range(NU + 1):
        half = 2 * (unit_cols(*UNITS[u])[1] + P * is_diag(*UNITS[u])) if u < NU else 0
        if u < NU:
            cost += [half, half]
        cost.append(PV_COLS * unit_cols(*UNITS[u - 1])[1] if u else 0)
    pcost = [p[3] * p[4] for p in PIECES]
    out, acc, pacc, done = [], 0, 0, 0
    for c in cost:
        acc += c
        while done < NP and (pacc + pcost[done]) * sum(cost) <= acc * sum(pcost) * EARLY:
            pacc += pcost[done]
            done += 1
        out.append(done)
    out[-1] = NP
    return out


PV_COLS = 4.3
EARLY = 1.02
SLOTS = piece_schedule()


def slot_pieces(slot):
    return range(SLOTS[slot - 1] if slot else 0, SLOTS[slot])


U_M1 = 1
U_O0 = 6
U_M0 = next(u for u in range(NU) if SLOTS[3 * u + 2] >= NP0) + 1


def build(nc, x_in, w_qkv, q_w, q_b, k_w, k_b, w_out, lora_a, lora_b, ffn_w, ffn_bias, lora_w, alibi, out):
    with ExitStack() as ctx:
        sem = lambda name: ctx.enter_context(nc.semaphore(name))
        sb = lambda name, shape, dt: ctx.enter_context(nc.sbuf_tensor(name, shape, dt))
        scratch = {(t, part): nc.dram_tensor(f"{t}{part + 1}_scratch", [B, D, S], BF16, kind="Internal").ap()
                   for t in "qk" for part in range(PARTS)}

        bank = [ctx.enter_context(nc.psum_tensor(f"bank{i}", [P, 512], F32)) for i in range(4)]
        score_t = ctx.enter_context(nc.psum_tensor("score_t", [P, 4, 512], F32))

        v_all = sb("v_all", [P, QUADS, SB, QH * HD], F32)
        z_all = sb("z_all", [P, TILES, D], F32)
        ident = sb("ident", [P, P], F32)
        ident_b = sb("ident_b", [P, P], BF16)
        mask_b = sb("mask_b", [P, P], BF16)

        project_stage(nc, sem, bank, score_t, scratch, v_all, z_all, ident, ident_b, mask_b,
                      x_in, w_qkv, q_w, q_b, k_w, k_b, lora_a, lora_b, ffn_w, ffn_bias, lora_w)
        attn = v_all
        wo_hi = sb("wo_hi", [P, DC, D], F32R)
        wo_lo = sb("wo_lo", [P, DC, D], F32R)
        attend_stage(nc, sem, bank, score_t, scratch, alibi, v_all, ident, ident_b, mask_b, attn, w_out, wo_hi, wo_lo)
        combine_stage(nc, sem, bank, x_in, wo_hi, wo_lo, z_all, attn, ident, out)


def project_stage(nc, sem, bank, score_t, scratch, v_all, z_all, ident, ident_b, mask_b,
                  x_in, w_qkv, q_w, q_b, k_w, k_b, lora_a, lora_b, ffn_w, ffn_bias, lora_w):
    WG = 4
    with ExitStack() as ctx:
        sb = lambda name, shape, dt: ctx.enter_context(nc.sbuf_tensor(name, shape, dt))
        wt_hi = sb("wt_hi", [P, DC, WG * D], F32R)
        wt_lo = sb("wt_lo", [P, DC, WG * D], F32R)
        w_raw = [sb(f"w_raw{i}", [P, 4, D], F32) for i in range(2)]
        xt = sb("xt", [P, GT, D], F32)
        xT_hi = [sb(f"xT_hi{i}", [P, DC, P], F32R) for i in range(2)]
        xT_lo = [sb(f"xT_lo{i}", [P, DC, P], F32R) for i in range(2)]
        qk = [sb(f"qk{i}", [P, 2, 2, D], F32) for i in range(2)]
        full = [sb(f"full{i}", [P, 2, 2 * P], F32) for i in range(2)]
        rest = [sb(f"rest{i}", [P, 2, 2 * P], F32) for i in range(2)]
        part = [[sb(f"part{x + 1}_{i}", [P, 2, 2 * P], BF16) for i in range(2)] for x in range(PARTS)]
        bias_bc = sb("bias_bc", [P, D], F32)
        la = sb("la", [P, D], F32)
        lb = sb("lb", [P, DC, NR * LR], F32)
        lbt = sb("lbt", [P, D], F32)
        lwb = sb("lwb", [P, NR], F32)
        ln_w = sb("ln_w", [P, 2, DC], F32)
        ln_b = sb("ln_b", [P, 2, DC], F32)
        eps = sb("eps", [P, 1], F32)
        st = sb("st", [P, 3, 6], F32)
        mv = sb("mv", [P, 3, 2], F32)
        sd = sb("sd", [P, 3], F32)
        rs = sb("rs", [P, 3], F32)

        consts = sem("consts")
        x_in_sem = [sem(f"x_loaded{i}") for i in range(GT)]
        w_in_sem = [sem(f"w_loaded{i}") for i in range(2)]
        small_in = sem("small_loaded")
        lb_scaled = sem("lora_b_scaled")
        ln_scaled = sem("ln_scaled")
        lb_turned = sem("lora_b_turned")
        lbt_ready = sem("lora_bt_ready")
        w_turned = sem("w_turned")
        w_hi_done = sem("w_hi_done")
        w_lo_done = sem("w_lo_done")
        x_stat = sem("x_stat")
        x_sd = sem("x_sd")
        x_norm = sem("x_norm")
        x_turned = sem("x_turned")
        x_hi = sem("x_hi")
        x_lo = sem("x_lo")
        q_out = sem("q_out")
        k_out = sem("k_out")
        v_out = sem("v_out")
        z_out = sem("z_out")
        qk_clip = sem("qk_clip")
        v_done = sem("v_done")
        z_done = sem("z_done")
        qk_stat = sem("qk_stat")
        qk_sd = sem("qk_sd")
        qk_norm = sem("qk_norm")
        qk_turned = sem("qk_turned")
        qk_full = sem("qk_full")
        qk_p1 = sem("qk_part1")
        qk_rest = sem("qk_rest")
        qk_p2 = sem("qk_part2")
        qk_p3 = sem("qk_part3")
        qk_store = [sem(f"qk_stored{i}") for i in range(2)]
        waited = sem("waited")
        dve = sem("dve_chain")
        turn_bank = [bank[0], bank[1]]
        out_bank = [score_t[:, i, :] for i in range(4)]
        qk_bank = [bank[2], bank[3]]
        xr = x_in.rearrange("b (t p) d -> (b t) p d", p=P)
        w_src = [w_qkv[g * D:(g + 1) * D, :] for g in range(3)] + [ffn_w]
        UP = 4
        SMALL = 16 * (1 + DC + 2 + 4 * DC)
        FULL0, P3_0, STORE0 = 4, 2, 48
        vt = v_all[:, :, :, :].rearrange("p (b m) k f -> p b m k f", b=B)

        def groups(eng, body):
            body(0, True, False)
            with eng.Fori(1, GROUPS - 1) as g:
                body(g, False, False)
            body(GROUPS - 1, False, True)

        def units(g, t, first, unit):
            if not (first and t < 2):
                for x in range(2):
                    k = 2 * (t % 2) + x
                    unit((g * 2 + t // 2 - 1) * UP + k, k % 2, k, 1 - t // 2)

        with nc.Block() as block:
            @block.sync
            def _(sp):
                for t in range(GT):
                    sp.dma_start(xt[:, t, :], xr[t]).then_inc(x_in_sem[t], 16)
                sp.dma_start(w_raw[0][:, :, :], w_src[0].rearrange("(t p) d -> p t d", p=P)).then_inc(w_in_sem[0], 16)
                sp.dma_start(w_raw[1][:, :, :], w_src[1].rearrange("(t p) d -> p t d", p=P)).then_inc(w_in_sem[1], 16)
                sp.dma_start(la[:, :], lora_a.rearrange("n r d -> (n r) d")).then_inc(small_in, 16)
                for t in range(DC):
                    sp.dma_start(lb[:, t, :].rearrange("p (n r) -> p n r", n=NR),
                                 lora_b[:, t * P:(t + 1) * P, :].rearrange("n p r -> p n r")).then_inc(small_in, 16)
                sp.dma_start(lwb[:, :], lora_w.rearrange("(a n) -> a n", a=1).broadcast_to([P, NR])).then_inc(small_in, 16)
                sp.dma_start(bias_bc[:, :], ffn_bias.rearrange("(a n) -> a n", a=1).broadcast_to([P, D])).then_inc(small_in, 16)
                for i, (w, b) in enumerate(((q_w, q_b), (k_w, k_b))):
                    for c in range(DC):
                        sp.dma_start(ln_w[:, i, c:c + 1], w[c * P:(c + 1) * P].rearrange("(p a) -> p a", a=1)).then_inc(small_in, 16)
                        sp.dma_start(ln_b[:, i, c:c + 1], b[c * P:(c + 1) * P].rearrange("(p a) -> p a", a=1)).then_inc(small_in, 16)
                for g in (2, 3):
                    sp.wait_ge(w_turned, DC * (g - 1))
                    sp.dma_start(w_raw[g % 2][:, :, :], w_src[g].rearrange("(t p) d -> p t d", p=P)).then_inc(w_in_sem[g % 2], 16)

                def store(n, par, k, pair_par):
                    t, c0 = "qk"[k // 2], 2 * (k % 2)
                    row, tok = (n >> 4) % B, (n >> 2) % 4
                    for x, (ready, start) in enumerate(((qk_p1, 0), (qk_p2, 0), (qk_p3, P3_0))):
                        sp.wait_ge(ready, n + 1 + start)
                        dst = scratch[t, x][bass.ds(row, 1), c0 * P:(c0 + 2) * P, bass.ds(tok * 2 * P, 2 * P)]
                        sp.dma_start(dst.rearrange("a (c p) t -> p (a c) t", p=P), part[x][par][:, :, :])\
                          .then_inc(qk_store[par], 16)

                def body(g, first, last):
                    for t in range(GT):
                        if not last:
                            sp.wait_ge(x_turned, g * GT + t + 1)
                            sp.dma_start(xt[:, t, :], xr[bass.ds(g * GT + GT + t, 1)].rearrange("a p d -> (a p) d")).then_inc(x_in_sem[t], 16)
                        units(g, t, first, store)
                groups(sp, body)
                for k in range(UP):
                    store((2 * GROUPS - 1) * UP + k, k % 2, k, 1)
                for i in range(2):
                    sp.wait_ge(qk_store[i], 16 * PARTS * UP * GROUPS + STORE0)

            @block.gpsimd
            def _(pool):
                pool.memset(eps[:, :], LN_EPS).then_inc(consts, 1)
                for m, v in ((ident, 0.0), (ident_b, 0.0), (mask_b, 0.0)):
                    pool.memset(m[:, :], v).then_inc(consts, 1)
                pool.wait_ge(consts, 4)
                for m in (ident, ident_b):
                    pool.affine_select(out=m[:, :], in_=m[:, :], compare_op=ALU.not_equal, fill=1.0, base=0,
                                       pattern=[[-1, P]], channel_multiplier=1).then_inc(consts, 1)
                pool.affine_select(out=mask_b[:, :], in_=mask_b[:, :], compare_op=ALU.is_ge, fill=MASKED, base=0,
                                   pattern=[[-1, P]], channel_multiplier=1).then_inc(consts, 1)
                pool.sem_inc(qk_p3, P3_0)
                for i in range(2):
                    pool.sem_inc(qk_store[i], STORE0)

                def unit(n, par, k, pair_par):
                    pool.wait_ge(qk_p1, n + 1)
                    pool.tensor_tensor(rest[par][:, :, :], full[par][:, :, :], part[0][par][:, :, :], ALU.subtract).then_inc(qk_rest, 1)
                    pool.wait_ge(qk_p2, n + 1)
                    pool.tensor_tensor(part[2][par][:, :, :], rest[par][:, :, :], part[1][par][:, :, :], ALU.subtract).then_inc(qk_p3, 1)

                def body(g, first, last):
                    for t in range(GT):
                        units(g, t, first, unit)
                groups(pool, body)
                for k in range(UP):
                    unit((2 * GROUPS - 1) * UP + k, k % 2, k, 1)

            @block.scalar
            def _(act):
                act.sem_inc(qk_full, FULL0)
                for n in range(WG * DC):
                    g, dc = n // DC, n % DC
                    act.wait_ge(w_turned, n + 1)
                    act.activation(wt_hi[:, dc, g * D:(g + 1) * D], qk_bank[n % 2][:, :], ACT.Copy).then_inc(w_hi_done, 1)

                def x_deviation(n):
                    act.wait_ge(x_stat, n + 1)
                    act.activation(sd[:, 2:3], mv[:, 2, 1:2], ACT.Sqrt, bias=eps[:, 0:1]).then_inc(x_sd, 1)

                def x_split(n, par):
                    act.wait_ge(x_turned, n + 1)
                    act.activation(xT_hi[par][:, :, :], turn_bank[par][:, :].rearrange("p (c t) -> p c t", c=DC),
                                   ACT.Copy).then_inc(x_hi, 1)

                act.wait_ge(consts, 7)
                x_deviation(0)
                x_split(0, 0)
                act.wait_ge(small_in, SMALL)
                act.wait_ge(ln_scaled, 1)

                def unit(n, par, k, pair_par):
                    i = k // 2
                    act.wait_ge(qk_turned, n + 1)
                    act.wait_ge(qk_p3, n - 1 + P3_0)
                    act.wait_ge(qk_store[par], (n >> 1) * 48 + STORE0)
                    for x in range(2):
                        c = 2 * (k % 2) + x
                        act.activation(full[par][:, x, :], qk_bank[par][:, x * 2 * P:(x + 1) * 2 * P], ACT.Identity,
                                       bias=ln_b[:, i, c:c + 1], scale=ln_w[:, i, c:c + 1]).then_inc(qk_full, 1)
                    act.wait_ge(qk_full, 2 * n + 2 + FULL0)
                    act.activation(part[0][par][:, :, :], full[par][:, :, :], ACT.Copy).then_inc(qk_p1, 1)

                def body(g, first, last):
                    for t in range(GT):
                        n = g * GT + t
                        nxt = not (last and t == GT - 1)
                        if nxt:
                            x_deviation(n + 1)
                        units(g, t, first, unit)
                        act.wait_ge(qk_stat, n + 1)
                        act.activation(sd[:, 0:2], mv[:, 0:2, 1], ACT.Sqrt, bias=eps[:, 0:1]).then_inc(qk_sd, 1)
                        if nxt:
                            x_split(n + 1, (t + 1) % 2)
                groups(act, body)
                for k in range(UP):
                    unit((2 * GROUPS - 1) * UP + k, k % 2, k, 1)

            @block.tensor
            def _(pe):
                pe.wait_ge(consts, 7)

                def turn_weights(n):
                    g, dc = n // DC, n % DC
                    if dc == 0:
                        pe.wait_ge(w_in_sem[g % 2], 16 * (g // 2 + 1))
                    if n >= 2:
                        pe.wait_ge(w_hi_done, n - 1)
                        pe.wait_ge(w_lo_done, n - 1)
                    dst = qk_bank[n % 2]
                    if g < 3:
                        for t in range(4):
                            mm = pe.transpose(dst[:, t * P:(t + 1) * P], w_raw[g % 2][:, t, dc * P:(dc + 1) * P], ident[:, :])
                    else:
                        pe.wait_ge(lbt_ready, 1)
                        pe.matmul(dst[:, :], la[:, dc * P:(dc + 1) * P], lbt[:, :], start=True, stop=False)
                        for t in range(4):
                            mm = pe.matmul(dst[:, t * P:(t + 1) * P], w_raw[g % 2][:, t, dc * P:(dc + 1) * P], ident[:, :],
                                           start=False, stop=(t == 3))
                    mm.then_inc(w_turned, 1)

                def turn_x(n, t):
                    pe.wait_ge(x_norm, n + 1)
                    for c in range(DC):
                        mm = pe.transpose(turn_bank[t % 2][:, c * P:(c + 1) * P], xt[:, t, c * P:(c + 1) * P], ident[:, :])
                    mm.then_inc(x_turned, 1)

                def project(n, t, which, signal):
                    wcols = slice(which * D, (which + 1) * D)
                    terms = [(xT_hi, wt_hi), (xT_hi, wt_lo), (xT_lo, wt_hi)]
                    for j, (a, w) in enumerate(terms):
                        for c in range(DC):
                            mm = pe.matmul(out_bank[which], a[t % 2][:, c, :], w[:, c, wcols],
                                           start=(j == 0 and c == 0), stop=(j == 2 and c == DC - 1))
                    mm.then_inc(signal, 1)

                pe.wait_ge(lb_scaled, 1)
                for t in range(DC):
                    mm = pe.transpose(turn_bank[1][:, t * P:(t + 1) * P], lb[:, t, :], ident[:, :])
                mm.then_inc(lb_turned, 1)
                for n in range(WG * DC):
                    turn_weights(n)
                pe.wait_ge(lbt_ready, 1)
                turn_x(0, 0)
                pe.wait_ge(w_hi_done, WG * DC)
                pe.wait_ge(w_lo_done, WG * DC)

                def unit(n, par, k, pair_par):
                    pe.wait_ge(qk_norm, (n >> 2) * 2 + 2)
                    pe.wait_ge(qk_full, 2 * n - 2 + FULL0)
                    for x in range(2):
                        c = 2 * (k % 2) + x
                        for t in range(2):
                            mm = pe.transpose(qk_bank[par][:, (2 * x + t) * P:(2 * x + t + 1) * P],
                                              qk[pair_par][:, k // 2, t, c * P:(c + 1) * P], ident[:, :])
                    mm.then_inc(qk_turned, 1)

                def body(g, first, last):
                    for t in range(GT):
                        n = g * GT + t
                        todo = []
                        units(g, t, first, lambda *args: todo.append(args))
                        pe.wait_ge(x_hi, n + 1)
                        pe.wait_ge(x_lo, n + 1)
                        pe.wait_ge(qk_clip, 2 * n + 1)
                        project(n, t, 0, q_out)
                        if todo:
                            unit(*todo[0])
                        pe.wait_ge(qk_clip, 2 * n + 2)
                        project(n, t, 1, k_out)
                        if todo:
                            unit(*todo[1])
                        pe.wait_ge(v_done, n + 1)
                        project(n, t, 2, v_out)
                        if not (last and t == GT - 1):
                            turn_x(n + 1, (t + 1) % GT)
                        pe.wait_ge(z_done, n + 1)
                        project(n, t, 3, z_out)
                groups(pe, body)
                for k in range(UP):
                    unit((2 * GROUPS - 1) * UP + k, k % 2, k, 1)

            @block.vector
            def _(v):
                v.sem_inc(qk_clip, 2)
                v.sem_inc(v_done, 1)
                v.sem_inc(z_done, 1)
                v.wait_ge(small_in, SMALL)
                for t in range(DC):
                    lbv = lb[:, t, :].rearrange("p (n r) -> p n r", n=NR)
                    ins = v.tensor_tensor(lbv, lbv, lwb[:, :].unsqueeze(2).broadcast_to([P, NR, LR]), ALU.mult)
                ins.then_inc(lb_scaled, 1)
                for par in (ln_w, ln_b):
                    ins = v.tensor_scalar(par[:, 0, :], par[:, 0, :], HD ** -0.5, None, ALU.mult)
                ins.then_inc(ln_scaled, 1)
                v.wait_ge(lb_turned, 1)
                v.tensor_scalar(lbt[:, :], turn_bank[1][:, :], LORA_SCALE, None, ALU.mult).then_inc(lbt_ready, 1)
                for n in range(WG * DC):
                    g, dc = n // DC, n % DC
                    v.wait_ge(w_hi_done, n + 1)
                    v.tensor_tensor(wt_lo[:, dc, g * D:(g + 1) * D], qk_bank[n % 2][:, :],
                                    wt_hi[:, dc, g * D:(g + 1) * D].bitcast(F32), ALU.subtract).then_inc(w_lo_done, 1)

                CHAIN = 5
                chained = [0]

                def chain(ins, base):
                    chained[0] += 1
                    ins.then_inc(dve, 1)
                    v.wait_ge(dve, base + chained[0])

                def stats(slot, src, base):
                    chain(v.bn_stats(st[:, slot, :], src), base)
                    v.sem_inc(waited, 1)
                    return v.bn_aggr(mv[:, slot, :], st[:, slot, :])

                def x_stats(t, k, base):
                    v.wait_ge(x_in_sem[t], 16 * k)
                    stats(2, xt[:, t, :], base).then_inc(x_stat, 1)

                def x_normalise(n, t, base):
                    v.wait_ge(x_sd, n + 1)
                    chain(v.reciprocal(rs[:, 2:3], sd[:, 2:3]), base)
                    v.tensor_scalar(xt[:, t, :], xt[:, t, :], mv[:, 2, 0:1], rs[:, 2:3], ALU.subtract, ALU.mult).then_inc(x_norm, 1)

                def x_split(n, par):
                    v.wait_ge(x_hi, n + 1)
                    v.tensor_tensor(xT_lo[par][:, :, :], turn_bank[par][:, :].rearrange("p (c t) -> p c t", c=DC),
                                    xT_hi[par][:, :, :].bitcast(F32), ALU.subtract).then_inc(x_lo, 1)

                x_stats(0, 1, 0)
                x_normalise(0, 0, 0)
                x_split(0, 0)
                before = chained[0]

                def part2(n, par, k, pair_par):
                    v.wait_ge(qk_rest, n + 1)
                    v.tensor_copy(part[1][par][:, :, :], rest[par][:, :, :]).then_inc(qk_p2, 1)

                def body(g, first, last):
                    for t in range(GT):
                        n = g * GT + t
                        nxt = not (last and t == GT - 1)
                        base = n * CHAIN + before
                        todo = []
                        units(g, t, first, lambda *args: todo.append(args))
                        pair = qk[t // 2]
                        chained[0] = 0
                        if nxt:
                            x_stats((t + 1) % GT, g + 1 + (t + 1) // GT, base)
                        for i, ready in ((0, q_out), (1, k_out)):
                            v.wait_ge(ready, n + 1)
                            v.tensor_scalar(pair[:, i, t % 2, :], out_bank[i], -CLIP, CLIP, ALU.max, ALU.min).then_inc(qk_clip, 1)
                            v.wait_ge(qk_clip, 2 * n + i + 3)
                            agg = stats(i, pair[:, i, t % 2, :], base)
                            if i:
                                agg.then_inc(qk_stat, 1)
                            if todo:
                                part2(*todo[i])
                        if nxt:
                            x_normalise(n + 1, (t + 1) % GT, base)
                        v.wait_ge(v_out, n + 1)
                        half = g >> 1
                        dst = vt[:, bass.ds(half, 1), :, bass.ds((g % 2) * GT + t, 1), :].rearrange("p a m k f -> p (a m k) f")
                        v.tensor_scalar(dst, out_bank[2].rearrange("p (m f) -> p m f", f=QH * HD), -CLIP, CLIP,
                                        ALU.max, ALU.min).then_inc(v_done, 1)
                        if nxt:
                            x_split(n + 1, (t + 1) % 2)
                        v.wait_ge(qk_sd, n + 1)
                        chain(v.reciprocal(rs[:, 0:2], sd[:, 0:2]), base)
                        for i in range(2):
                            ins = v.tensor_scalar(pair[:, i, t % 2, :], pair[:, i, t % 2, :], mv[:, i, 0:1], rs[:, i:i + 1],
                                                  ALU.subtract, ALU.mult)
                        ins.then_inc(qk_norm, 1)
                        v.wait_ge(z_out, n + 1)
                        v.tensor_tensor(z_all[:, bass.ds(n, 1), :].rearrange("p a d -> p (a d)"), out_bank[3], bias_bc[:, :],
                                        ALU.add).then_inc(z_done, 1)
                groups(v, body)
                for k in range(UP):
                    part2((2 * GROUPS - 1) * UP + k, k % 2, k, 1)


def attend_stage(nc, sem, bank, score_t, scratch, alibi, v_all, ident, ident_b, mask_b, attn, w_out, wo_hi, wo_lo):
    with ExitStack() as ctx:
        sb = lambda name, shape, dt: ctx.enter_context(nc.sbuf_tensor(name, shape, dt))
        qT = [sb(f"qT{i}", [P, QH, S], BF16) for i in range(BUFS)]
        kT = [sb(f"kT{i}", [P, QH, S], BF16) for i in range(BUFS)]
        vq = [sb(f"vq{i}", [P, SB, QH, 32], F32) for i in range(BUFS)]
        prob = [sb(f"prob{i}", [P, QH, CW], F32) for i in range(3)]
        oT = [sb(f"oT{i}", [P, CW], F32) for i in range(2)]
        top = sb("top", [P, 2, SB, QH], F32)
        mrest = sb("mrest", [P, 4, QH], F32)
        msplit = [sb(f"msplit{i}", [P, 4, QH, PARTS], BF16) for i in range(2)]
        mrow = [sb(f"mrow{i}", [QH * PARTS, CW], BF16) for i in range(2)]
        inv = sb("inv", [P, 4, QH], F32)
        ones = sb("ones", [PARTS, QH, S], BF16)
        wo_raw = sb("wo_raw", [P, 4, D], F32)
        alibi_b = alibi.bitcast(BF16)

        score_q = [bank[0], bank[1]]
        out_t = bank[2]
        turn = bank[3]
        turn_b = turn[:, :].bitcast(BF16)

        loaded = [sem(f"qk_loaded{i}") for i in range(BUFS)]
        ones_set = sem("ones_set")
        ones_in = sem("ones_in")
        quad_free = sem("quad_free")
        v_copied = sem("v_copied")
        piece_out = sem("piece_out")
        piece_max = sem("piece_max")
        top_done = sem("top_done")
        m_split = [sem(f"m_split{c}") for c in range(2)]
        m_chain = sem("m_chain")
        v_filled = sem("v_filled")
        turned = sem("turned")
        turn_free = sem("turn_free")
        m_rows = [sem(f"m_rows{c}") for c in range(2)]
        m_in = [sem(f"m_in{c}") for c in range(2)]
        st_out = sem("st_out")
        exp_done = sem("exp_done")
        pv_done = sem("pv_done")
        o_taken = sem("o_taken")
        inv_done = sem("inv_done")
        wo_in = sem("wo_loaded")
        wo_turned = sem("wo_turned")
        wo_hi_done = sem("wo_hi_done")
        wo_lo_done = sem("wo_lo_done")
        HU = 2 * NU
        LOADS = 16 * 2 * (len(TERMS) + 1)
        EXP0, PIECE0, PV0, FREE0, ROWS0, TURN0 = 2, 2, 3, 2, 64, 1

        wo_unit = {1: 0, 3: 1, 5: 2, 7: 3}

        def quads(eng, step):
            with eng.Fori(0, QUADS // BUFS - 1) as i:
                for s in range(BUFS):
                    step(i * BUFS + s, s, i, BUFS)
            for n in range(QUADS - QUADS % BUFS - BUFS, QUADS):
                step(n, n % BUFS, n // BUFS, QUADS - 1 - n)

        with nc.Block() as block:
            @block.sync
            def _(sp):
                def load(n, s):
                    for tile, t in ((kT[s], 1), (qT[s], 0)):
                        sp.dma_start(tile[0:N_ALIBI, :, :], alibi_b[t].rearrange("(m h) r s -> m r h s", h=QH)[bass.ds(n % (H // QH), 1)]
                                     .rearrange("a r h s -> (a r) h s")).then_inc(loaded[s], 16)
                        for k, term in enumerate(TERMS):
                            src = scratch["qk"[t], term[t]].rearrange("b (m h d) s -> (b m) d h s", h=QH, d=HD)
                            r0 = R_DOT + HD * k
                            sp.dma_start(tile[r0:r0 + HD, :, :], src[bass.ds(n, 1)].rearrange("a d h s -> (a d) h s"))\
                              .then_inc(loaded[s], 16)

                def send_rows(s, c):
                    for h in range(QH):
                        sp.dma_start(qT[s][R_MAX:K_EXP, h, c * CW:(c + 1) * CW], mrow[c][PARTS * h:PARTS * (h + 1), :])\
                          .then_inc(m_in[c], 16)

                load(0, 0)
                sp.wait_ge(ones_set, 1)
                for s in range(BUFS):
                    sp.dma_start(kT[s][R_MAX:K_EXP, :, :], ones[:, :, :]).then_inc(ones_in, 16)
                load(1, 1)
                sp.dma_start(wo_raw[:, :, :], w_out.rearrange("(t p) d -> p t d", p=P)).then_inc(wo_in, 16)
                sp.wait_ge(m_rows[0], 1)
                send_rows(0, 0)

                def step(n, s, i, left):
                    sp.wait_ge(m_rows[1], n + 1)
                    send_rows(s, 1)
                    if left >= 2:
                        sp.wait_ge(quad_free, n + FREE0)
                        load(n + 2, (s + 2) % BUFS)
                    if left >= 1:
                        sp.wait_ge(m_rows[0], n + 2)
                        send_rows((s + 1) % BUFS, 0)
                quads(sp, step)
                sp.wait_ge(m_in[0], 64 * QUADS)
                sp.wait_ge(m_in[1], 64 * QUADS + ROWS0)

            @block.gpsimd
            def _(pool):
                pool.sem_inc(m_in[1], ROWS0)
                pool.memset(ones[:, :, :], 1.0).then_inc(ones_set, 1)
                for i in range(BUFS):
                    pool.memset(vq[i][:, :, :, :], 1.0).then_inc(v_filled, 1)
                pool.wait_ge(v_filled, BUFS)

                def copy_v(n, s):
                    pool.tensor_copy(vq[s][:, :, :, 0:HD], v_all[:, bass.ds(n, 1), :, :]
                                     .rearrange("p a k (h d) -> p (a k) h d", h=QH)).then_inc(v_copied, 1)

                copy_v(0, 0)

                def step(n, s, i, left):
                    if left:
                        pool.wait_ge(quad_free, n - 1 + FREE0)
                        copy_v(n + 1, (s + 1) % BUFS)
                quads(pool, step)

            @block.scalar
            def _(act):
                act.sem_inc(exp_done, EXP0)

                def maxima_rows(c, wait_rows, use):
                    act.wait_ge(turned, use)
                    if wait_rows is not None:
                        act.wait_ge(m_in[c], wait_rows)
                    act.activation(mrow[c][:, :], turn_b[0:QH * PARTS, 0:CW], ACT.Copy).then_inc(m_rows[c], 1)

                maxima_rows(0, None, 1)

                def take_output(n, c):
                    last_unit = 4 * (c + 1) - 1 if c == 0 else NU - 1
                    act.wait_ge(pv_done, n * NU + last_unit + 1 + PV0)
                    act.activation(oT[c][:, :], out_t[:, :], ACT.Copy).then_inc(o_taken, 1)

                def step(n, s, i, left):
                    for u, (c, kb) in enumerate(UNITS):
                        _, w = unit_cols(c, kb)
                        for j in range(2):
                            act.wait_ge(st_out, n * HU + 2 * u + j + 1)
                            if j == 0:
                                act.wait_ge(pv_done, n * NU + u - 2 + PV0)
                            act.activation(prob[u % 3][:, 2 * j:2 * j + 2, 0:w], score_t[:, 2 * j:2 * j + 2, 0:w],
                                           ACT.Exp).then_inc(exp_done, 1)
                        if left == 0 and u in wo_unit:
                            dc = wo_unit[u]
                            act.wait_ge(wo_turned, dc + 1)
                            act.activation(wo_hi[:, dc, :], score_q[dc % 2][:, :], ACT.Copy).then_inc(wo_hi_done, 1)
                        if u == U_M1:
                            maxima_rows(1, n * 64 + ROWS0, n * 4 + 2)
                        if u == U_M0 and left:
                            maxima_rows(0, n * 64 + 64, n * 4 + 3)
                        if u == 4:
                            take_output(n, 0)
                    take_output(n, 1)
                quads(act, step)

            @block.tensor
            def _(pe):
                pe.sem_inc(pv_done, PV0)
                pe.sem_inc(quad_free, FREE0)

                def piece(q, s, p):
                    qb, kc, h0, nh, w = PIECES[p]
                    pe.wait_ge(piece_max, q * NP + p - 1 + PIECE0)
                    dst = score_q[p % 2]
                    for x in range(nh):
                        h = h0 + x
                        mm = pe.matmul(dst[:, x * w:(x + 1) * w], qT[s][0:K_MAX, h, qb * P:(qb + 1) * P],
                                       kT[s][0:K_MAX, h, kc * CW:kc * CW + w], start=True, stop=(kc != qb // 4))
                        if kc == qb // 4:
                            mm = pe.matmul(dst[:, (x + 1) * w - P:(x + 1) * w], ident_b[:, :], mask_b[:, :],
                                           start=False, stop=True)
                    mm.then_inc(piece_out, 1)

                def turn_maxima(c, q):
                    pe.wait_ge(m_split[c], q + 1)
                    for b in range(4):
                        mm = pe.transpose(turn_b[0:QH * PARTS, b * P:(b + 1) * P],
                                          msplit[c][:, b, :, :].rearrange("p h x -> p (h x)"), ident_b[:, :])
                    mm.then_inc(turned, 1)

                def turn_output(n, c):
                    pe.wait_ge(o_taken, 2 * n + c + 1)
                    for b in range(4):
                        mm = pe.transpose(turn[:, b * P:(b + 1) * P], oT[c][:, b * P:(b + 1) * P], ident[:, :])
                        if c == 1 and b == 0:
                            mm.then_inc(quad_free, 1)
                    mm.then_inc(turned, 1)

                def exponents(n, s, u, j):
                    c, kb = UNITS[u]
                    q0, w = unit_cols(c, kb)
                    pe.wait_ge(exp_done, n * HU + 2 * u + j - 1 + EXP0)
                    for h in range(2 * j, 2 * j + 2):
                        mm = pe.matmul(score_t[:, h, 0:w], kT[s][0:K_EXP, h, kb * P:(kb + 1) * P],
                                       qT[s][0:K_EXP, h, q0:q0 + w], start=True, stop=not is_diag(c, kb))
                        if is_diag(c, kb):
                            mm = pe.matmul(score_t[:, h, 0:P], mask_b[:, :], ident_b[:, :], start=False, stop=True)
                    mm.then_inc(st_out, 1)

                def apply_v(n, s, u):
                    c, kb = UNITS[u]
                    q0, w = unit_cols(c, kb)
                    pe.wait_ge(exp_done, n * HU + 2 * u + 2 + EXP0)
                    for h in range(QH):
                        mm = pe.matmul(out_t[32 * h:32 * h + 32, q0 - CW * c:q0 - CW * c + w], vq[s][:, kb, h, :],
                                       prob[u % 3][:, h, 0:w], start=(kb == 0), stop=(kb == 4 * (c + 1) - 1))
                    mm.then_inc(pv_done, 1)

                def turn_out_weights(dc):
                    if dc == 0:
                        pe.wait_ge(wo_in, 16)
                        pe.wait_ge(piece_max, QUADS * NP + PIECE0)
                    if dc >= 2:
                        pe.wait_ge(wo_lo_done, dc - 1)
                    for t in range(4):
                        mm = pe.transpose(score_q[dc % 2][:, t * P:(t + 1) * P], wo_raw[:, t, dc * P:(dc + 1) * P], ident[:, :])
                    mm.then_inc(wo_turned, 1)

                pe.wait_ge(loaded[0], LOADS)
                for p in range(NP):
                    piece(0, 0, p)
                turn_maxima(0, 0)
                pe.wait_ge(ones_in, 16 * BUFS)

                def step(n, s, i, left):
                    pe.wait_ge(m_in[0], n * 64 + 64)
                    pe.wait_ge(v_copied, n + 1)
                    nxt = (s + 1) % BUFS

                    def pieces(slot):
                        if left:
                            for p in slot_pieces(slot):
                                piece(n + 1, nxt, p)

                    for u in range(NU):
                        if UNITS[u] == (1, 0):
                            pe.wait_ge(m_in[1], n * 64 + 64 + ROWS0)
                        exponents(n, s, u, 0)
                        if left and u == 0:
                            pe.wait_ge(loaded[nxt], (i + 1 + (s + 1) // BUFS) * LOADS)
                        pieces(3 * u)
                        exponents(n, s, u, 1)
                        pieces(3 * u + 1)
                        if left == 0 and u in wo_unit:
                            turn_out_weights(wo_unit[u])
                        if u == U_M1:
                            pe.wait_ge(m_rows[0], n + 1)
                            pe.wait_ge(turn_free, n * 2 + TURN0)
                            turn_maxima(1, n)
                        if u == U_M0 and left:
                            pe.wait_ge(m_rows[1], n + 1)
                            turn_maxima(0, n + 1)
                        if u >= 1:
                            if u == 5:
                                pe.wait_ge(o_taken, 2 * n + 1)
                            apply_v(n, s, u - 1)
                        pieces(3 * u + 2)
                        if u == U_O0:
                            if left:
                                pe.wait_ge(m_rows[0], n + 2)
                            else:
                                pe.wait_ge(m_rows[1], n + 1)
                            turn_output(n, 0)
                    apply_v(n, s, NU - 1)
                    pieces(3 * NU)
                    pe.wait_ge(turn_free, n * 2 + 1 + TURN0)
                    turn_output(n, 1)
                quads(pe, step)

            @block.vector
            def _(v):
                v.sem_inc(piece_max, PIECE0)
                v.sem_inc(turn_free, TURN0)

                def maxima(q, p):
                    qb, kc, h0, nh, w = PIECES[p]
                    v.wait_ge(piece_out, q * NP + p + 1)
                    v.tensor_reduce(top[:, kc, qb, h0:h0 + nh], score_q[p % 2][:, 0:nh * w].rearrange("p (h w) -> p h w", w=w),
                                    AX.X, ALU.max).then_inc(piece_max, 1)

                def split(q, c, pieces):
                    v.wait_ge(piece_max, q * NP + pieces + PIECE0)
                    if c == 1:
                        v.tensor_tensor(top[:, 0, 4:8, :], top[:, 0, 4:8, :], top[:, 1, 4:8, :], ALU.max).then_inc(top_done, 1)
                        v.wait_ge(top_done, q + 1)
                    m = top[:, 0, 4 * c:4 * c + 4, :]
                    one, two, three = (msplit[c][:, :, :, x] for x in range(PARTS))
                    v.tensor_scalar(one, m, -1.0, None, ALU.mult).then_inc(m_chain, 1)
                    k = (2 * q + c) * 3
                    v.wait_ge(m_chain, k + 1)
                    v.scalar_tensor_tensor(out=mrest[:, :, :], in0=m, scalar=-1.0, in1=one, op0=ALU.mult, op1=ALU.subtract)\
                     .then_inc(m_chain, 1)
                    v.wait_ge(m_chain, k + 2)
                    v.tensor_copy(two, mrest[:, :, :]).then_inc(m_chain, 1)
                    v.wait_ge(m_chain, k + 3)
                    v.tensor_tensor(three, mrest[:, :, :], two, ALU.subtract).then_inc(m_split[c], 1)

                def normalise(n, c, use):
                    v.wait_ge(turned, use)
                    o = turn[:, :].rearrange("p (b h x) -> p b h x", b=4, h=QH)
                    v.reciprocal(inv[:, :, :], o[:, :, :, HD]).then_inc(inv_done, 1)
                    v.wait_ge(inv_done, 2 * n + c + 1)
                    dst = attn[:, bass.ds(n, 1), 4 * c:4 * c + 4, :].rearrange("p a b (h d) -> p (a b) h d", h=QH)
                    v.tensor_tensor(dst, o[:, :, :, 0:HD], inv[:, :, :].unsqueeze(3).broadcast_to([P, 4, QH, HD]),
                                    ALU.mult).then_inc(turn_free, 1)

                for p in range(NP):
                    maxima(0, p)
                    if p == NP0 - 1:
                        split(0, 0, NP0)
                split(0, 1, NP)

                def step(n, s, i, left):
                    def pieces(slot):
                        if left:
                            for p in slot_pieces(slot):
                                maxima(n + 1, p)
                                if p == NP0 - 1:
                                    split(n + 1, 0, NP0)

                    for u in range(NU):
                        for k in range(3):
                            pieces(3 * u + k)
                        if left == 0 and u in wo_unit:
                            dc = wo_unit[u]
                            v.wait_ge(wo_hi_done, dc + 1)
                            v.tensor_tensor(wo_lo[:, dc, :], score_q[dc % 2][:, :], wo_hi[:, dc, :].bitcast(F32), ALU.subtract)\
                             .then_inc(wo_lo_done, 1)
                        if u == U_O0:
                            normalise(n, 0, n * 4 + (4 if left else 3))
                    pieces(3 * NU)
                    if left:
                        split(n + 1, 1, NP)
                    normalise(n, 1, n * 4 + (5 if left else 4))
                quads(v, step)


def combine_stage(nc, sem, bank, x_in, wo_hi, wo_lo, z_all, attn, ident, out):
    with ExitStack() as ctx:
        sb = lambda name, shape, dt: ctx.enter_context(nc.sbuf_tensor(name, shape, dt))
        at = [sb(f"at{i}", [P, D], F32) for i in range(2)]
        aT_hi = [sb(f"aT_hi{i}", [P, DC, P], F32R) for i in range(2)]
        aT_lo = [sb(f"aT_lo{i}", [P, DC, P], F32R) for i in range(2)]
        xc = [sb(f"xc{i}", [P, D], F32) for i in range(2)]
        gate = [sb(f"gate{i}", [P, D], F32) for i in range(2)]
        prod = [sb(f"prod{i}", [P, D], F32) for i in range(2)]
        y = [sb(f"y{i}", [P, D], F32) for i in range(2)]
        turn_bank, out_bank = [bank[0], bank[1]], [bank[2], bank[3]]

        x_loaded = [sem(f"xc_loaded{i}") for i in range(2)]
        staged = sem("staged")
        a_turned = sem("a_turned")
        a_hi = sem("a_hi")
        a_lo = sem("a_lo")
        projected = sem("projected")
        gated = sem("gated")
        multiplied = sem("multiplied")
        y_done = sem("y_done")
        y_stored = [sem(f"y_stored{i}") for i in range(2)]
        xr = x_in.rearrange("b (t p) d -> (b t) p d", p=P)
        yr = out.rearrange("b (t p) d -> (b t) p d", p=P)
        av = attn[:, :, :, :].rearrange("p (b m) k f -> p b m k f", b=B)
        TB = 4
        A0, Y0, MUL0 = 1, 2, 2

        def tiles(eng, step):
            with eng.Fori(0, TILES // TB - 1) as i:
                for t in range(TB):
                    step(i * TB + t, i, t, TB)
            i = TILES // TB - 1
            for t in range(TB):
                step(i * TB + t, i, t, TB - 1 - t)

        with nc.Block() as block:
            @block.sync
            def _(sp):
                for t in range(2):
                    sp.dma_start(xc[t][:, :], xr[t]).then_inc(x_loaded[t], 16)

                def step(n, i, t, left):
                    sp.wait_ge(y_done, n + 1 + Y0)
                    sp.dma_start(yr[bass.ds(n, 1)].rearrange("a p d -> (a p) d"), y[t % 2][:, :]).then_inc(y_stored[t % 2], 16)
                    if left >= 2:
                        sp.dma_start(xc[t % 2][:, :], xr[bass.ds(n + 2, 1)].rearrange("a p d -> (a p) d")).then_inc(x_loaded[t % 2], 16)
                tiles(sp, step)
                for t in range(2):
                    sp.wait_ge(y_stored[t], 16 * TILES // 2 + 16)

            @block.gpsimd
            def _(pool):
                def stage(n, i, t):
                    half = (i >> 1) % B
                    pool.tensor_copy(at[t % 2][:, :].rearrange("p (m f) -> p m f", f=QH * HD),
                                     av[:, bass.ds(half, 1), :, bass.ds((i % 2) * TB + t, 1), :]
                                     .rearrange("p a m k f -> p (a m k) f")).then_inc(staged, 1)

                stage(0, 0, 0)

                def step(n, i, t, left):
                    if left:
                        pool.wait_ge(a_turned, n + A0)
                        stage(n + 1, i + (t + 1) // TB, (t + 1) % TB)
                tiles(pool, step)

            @block.scalar
            def _(act):
                def cut(n, t):
                    act.wait_ge(a_turned, n + 1 + A0)
                    act.activation(aT_hi[t % 2][:, :, :], turn_bank[t % 2][:, :].rearrange("p (c t) -> p c t", c=DC),
                                   ACT.Copy).then_inc(a_hi, 1)

                cut(0, 0)

                def step(n, i, t, left):
                    act.wait_ge(y_done, n - 1 + Y0)
                    act.activation(gate[t % 2][:, :], z_all[:, bass.ds(n, 1), :].rearrange("p a d -> p (a d)"),
                                   ACT.Silu).then_inc(gated, 1)
                    if left:
                        cut(n + 1, t + 1)
                tiles(act, step)

            @block.tensor
            def _(pe):
                pe.sem_inc(a_turned, A0)

                def turn_tile(n, t):
                    pe.wait_ge(staged, n + 1)
                    for c in range(DC):
                        mm = pe.transpose(turn_bank[t % 2][:, c * P:(c + 1) * P], at[t % 2][:, c * P:(c + 1) * P], ident[:, :])
                    mm.then_inc(a_turned, 1)

                turn_tile(0, 0)

                def step(n, i, t, left):
                    if left:
                        turn_tile(n + 1, t + 1)
                    pe.wait_ge(a_hi, n + 1)
                    pe.wait_ge(a_lo, n + 1)
                    pe.wait_ge(multiplied, n - 1 + MUL0)
                    for j, (a, w) in enumerate([(aT_hi, wo_hi), (aT_hi, wo_lo), (aT_lo, wo_hi)]):
                        for c in range(DC):
                            mm = pe.matmul(out_bank[t % 2][:, :], a[t % 2][:, c, :], w[:, c, :],
                                           start=(j == 0 and c == 0), stop=(j == 2 and c == DC - 1))
                    mm.then_inc(projected, 1)
                tiles(pe, step)

            @block.vector
            def _(v):
                v.sem_inc(multiplied, MUL0)
                v.sem_inc(y_done, Y0)
                for t in range(2):
                    v.sem_inc(y_stored[t], 16)

                def cut(n, t):
                    v.wait_ge(a_hi, n + 1)
                    v.tensor_tensor(aT_lo[t % 2][:, :, :], turn_bank[t % 2][:, :].rearrange("p (c t) -> p c t", c=DC),
                                    aT_hi[t % 2][:, :, :].bitcast(F32), ALU.subtract).then_inc(a_lo, 1)

                cut(0, 0)

                def step(n, i, t, left):
                    if left:
                        cut(n + 1, t + 1)
                    v.wait_ge(projected, n + 1)
                    v.wait_ge(gated, n + 1)
                    v.tensor_tensor(prod[t % 2][:, :], out_bank[t % 2][:, :], gate[t % 2][:, :], ALU.mult).then_inc(multiplied, 1)
                    v.wait_ge(multiplied, n + 1 + MUL0)
                    v.wait_ge(x_loaded[t % 2], (i * 2 + t // 2) * 16 + 16)
                    v.wait_ge(y_stored[t % 2], (i * 2 + t // 2) * 16 + 16)
                    v.tensor_tensor(y[t % 2][:, :], prod[t % 2][:, :], xc[t % 2][:, :], ALU.add).then_inc(y_done, 1)
                tiles(v, step)


_INS = ['L0_attn_hidden_states', 'L0_attn_w_qkv', 'L0_attn_q_ln_w', 'L0_attn_q_ln_b', 'L0_attn_k_ln_w', 'L0_attn_k_ln_b',
        'L0_attn_w_out', 'L0_ffn_lora_A', 'L0_ffn_lora_B', 'L0_ffn_W', 'L0_ffn_bias', 'L0_ffn_lora_weights']


def alibi_rows():
    import numpy as _np
    slopes = (_np.float32(1.0) / _np.power(_np.float32(2.0), _np.arange(1, H + 1, dtype=_np.float32) * _np.float32(8 / H)))
    pos = _np.arange(S, dtype=_np.float32)
    one = _np.ones(S, _np.float32)
    rows = _np.empty((2, H, N_ALIBI, S), _np.float32)
    for h in range(H):
        left = _np.float32(slopes[h])
        for x in range(PARTS):
            s = (left.reshape(1).view(_np.uint32) & _np.uint32(0xFFFF0000)).view(_np.float32)[0]
            left = left - s
            for y, p in enumerate((pos - pos % P, pos % P)):
                r = 4 * x + 2 * y
                rows[0, h, r], rows[1, h, r] = s * one, p
                rows[0, h, r + 1], rows[1, h, r + 1] = -p, s * one
    return (rows.view(_np.uint32) >> 16).astype(_np.uint16)


def kernel(**inputs):
    import numpy as _np
    import concourse.bacc as _bacc
    from concourse import mybir as _mybir
    from concourse.bass_utils import run_bass_kernel_spmd as _run

    nc = _bacc.Bacc("TRN2", target_bir_lowering=False, num_devices=1)
    arrays, args = {}, []
    for name in _INS:
        a = _np.ascontiguousarray(inputs[name])
        arrays[f"in_{name}_dram"] = a
        args.append(nc.dram_tensor(f"in_{name}_dram", a.shape, _mybir.dt.from_np(a.dtype), kind="ExternalInput").ap())
    rows = alibi_rows()
    arrays["alibi_dram"] = rows
    args.append(nc.dram_tensor("alibi_dram", rows.shape, _mybir.dt.uint16, kind="ExternalInput").ap())
    args.append(nc.dram_tensor("out_0_dram", (B, S, D), _mybir.dt.float32, kind="ExternalOutput").ap())
    build(nc, *args)
    r = _run(nc, [arrays], core_ids=[0])
    return r.results[0]["out_0_dram"]
```

```python
from contextlib import ExitStack

import concourse.bass as bass
from concourse import mybir

F32 = mybir.dt.float32
F32R = mybir.dt.float32r
BF16 = mybir.dt.bfloat16
ALU = mybir.AluOpType
ACT = mybir.ActivationFunctionType
AX = mybir.AxisListType

P = 128
B, S, D = 2, 1024, 512
H = 32
HD = D // H
DC = D // P
TILES = B * S // P
GT = 4
GROUPS = TILES // GT
SB = S // P
CLIP = 8.0
LN_EPS = 1e-5
NR, LR = 8, 16
LORA_SCALE = 32 / LR

QH = 4
QUADS = B * H // QH
BUFS = 3
PARTS = 3
N_ALIBI = 4 * PARTS
TERMS = [(0, 0), (0, 1), (0, 2), (1, 0), (1, 1), (2, 0)]
R_DOT = N_ALIBI
R_MAX = R_DOT + len(TERMS) * HD
K_MAX = R_MAX
K_EXP = R_MAX + PARTS
CW = 512
MASKED = -1e30
TB = 4

UNITS = [(c, kb) for c in range(2) for kb in range(4 * (c + 1))]
NU = len(UNITS)


def unit_cols(c, kb):
    q0 = max(CW * c, P * kb)
    return q0, CW * (c + 1) - q0


def is_diag(c, kb):
    return kb >= 4 * c


def max_pieces():
    out = []
    for qb in range(SB):
        for kc in range(qb // 4 + 1):
            w = min(CW, P * (qb + 1) - CW * kc)
            nh = {128: 4, 256: 2}.get(w, 1)
            out += [(qb, kc, h0, nh, w) for h0 in range(0, QH, nh)]
    return out


PIECES = max_pieces()
NP = len(PIECES)
NP0 = sum(p[0] < 4 for p in PIECES)


PIECES_IN_SLOT = [
    0, 0, 2,
    0, 2, 1,
    2, 2, 1,
    1, 0, 0,
    2, 0, 1,
    1, 2, 1,
    1, 1, 2,
    1, 1, 1,
    1, 1, 2,
    0, 2, 1,
    1, 1, 2,
    0, 0, 1,
    1
]
assert sum(PIECES_IN_SLOT) == NP and len(PIECES_IN_SLOT) == 3 * NU + 1
SLOTS = [sum(PIECES_IN_SLOT[:slot + 1]) for slot in range(3 * NU + 1)]


def slot_pieces(slot):
    return range(SLOTS[slot - 1] if slot else 0, SLOTS[slot])


U_M1 = 1
U_M0 = 4
U_O0 = 6
assert SLOTS[3 * U_M0 + 1] >= NP0


def build(nc, x_in, w_qkv, q_w, q_b, k_w, k_b, w_out, lora_a, lora_b, ffn_w, ffn_bias, lora_w, alibi, out):
    with ExitStack() as ctx:
        sem = lambda name: ctx.enter_context(nc.semaphore(name))
        sb = lambda name, shape, dt: ctx.enter_context(nc.sbuf_tensor(name, shape, dt))
        scratch = {(t, part): nc.dram_tensor(f"{t}{part + 1}_scratch", [B, D, S], BF16, kind="Internal").ap()
                   for t in "qk" for part in range(PARTS)}

        bank = [ctx.enter_context(nc.psum_tensor(f"bank{i}", [P, 512], F32)) for i in range(4)]
        score_t = ctx.enter_context(nc.psum_tensor("score_t", [P, 4, 512], F32))

        v_all = sb("v_all", [P, QUADS, SB, QH * HD], F32)
        z_all = sb("z_all", [P, TILES, D], F32)
        ident = sb("ident", [P, P], F32)
        ident_b = sb("ident_b", [P, P], BF16)
        mask_b = sb("mask_b", [P, P], BF16)

        qT0 = sb("qT0", [P, QH, S], BF16)
        kT0 = sb("kT0", [P, QH, S], BF16)
        ones = sb("ones", [PARTS, S], BF16)
        turner = Turner(nc, sem, sb, [bank[2], bank[3]], ident, scratch)
        quad_in = QuadLoads(sem, scratch, alibi, ones)
        project_stage(nc, sem, bank, score_t, turner, quad_in, v_all, z_all, ident, ident_b, mask_b, qT0, kT0, ones,
                      x_in, w_qkv, q_w, q_b, k_w, k_b, lora_a, lora_b, ffn_w, ffn_bias, lora_w)
        attn = v_all
        at = [turner.full[i][:, :, :].rearrange("p a t -> p (a t)") for i in range(2)]
        staged = sem("staged")
        av = attn[:, :, :, :].rearrange("p (b m) k f -> p b m k f", b=B)

        def stage(pool, n, i, t):
            pool.tensor_copy(at[t % 2].rearrange("p (m f) -> p m f", f=QH * HD),
                             av[:, bass.ds((i >> 1) % B, 1), :, bass.ds((i % 2) * TB + t, 1), :]
                             .rearrange("p a m k f -> p (a m k) f")).then_inc(staged, 1)

        wo_hi = sb("wo_hi", [P, DC, D], F32R)
        wo_lo = sb("wo_lo", [P, DC, D], F32R)
        attend_stage(nc, sem, bank, score_t, turner, quad_in, qT0, kT0, v_all, ident, ident_b, mask_b, attn, w_out, wo_hi, wo_lo, stage)
        combine_stage(nc, sem, bank, x_in, wo_hi, wo_lo, z_all, at, staged, stage, ident, out)


class Turner:
    UP = 4
    FULL0, P3_0, STORE0 = 4, 2, 48

    def __init__(self, nc, sem, sb, qk_bank, ident, scratch):
        self.nc, self.qk_bank, self.ident, self.scratch = nc, qk_bank, ident, scratch
        self.qk = [sb(f"qk{i}", [P, 2, 2, D], F32) for i in range(2)]
        self.full = [sb(f"full{i}", [P, 2, 2 * P], F32) for i in range(2)]
        self.rest = [sb(f"rest{i}", [P, 2, 2 * P], F32) for i in range(2)]
        self.part = [[sb(f"part{x + 1}_{i}", [P, 2, 2 * P], BF16) for i in range(2)] for x in range(PARTS)]
        self.ln = sb("ln", [P, 4, DC], F32)
        self.qk_norm = sem("qk_norm")
        self.qk_turned = sem("qk_turned")
        self.qk_full = sem("qk_full")
        self.qk_p1 = sem("qk_part1")
        self.qk_rest = sem("qk_rest")
        self.qk_p2 = sem("qk_part2")
        self.qk_p3 = sem("qk_part3")
        self.qk_store = [sem(f"qk_stored{i}") for i in range(2)]

    def tensor(self, pe, n, par, k, pair):
        pe.wait_ge(self.qk_norm, (n >> 2) * 2 + 2)
        pe.wait_ge(self.qk_full, 2 * n - 2 + self.FULL0)
        for x in range(2):
            c = 2 * (k % 2) + x
            for t in range(2):
                mm = pe.transpose(self.qk_bank[par][:, (2 * x + t) * P:(2 * x + t + 1) * P],
                                  self.qk[pair][:, k // 2, t, c * P:(c + 1) * P], self.ident[:, :])
        mm.then_inc(self.qk_turned, 1)

    def scalar(self, act, n, par, k, pair):
        i = k // 2
        act.wait_ge(self.qk_turned, n + 1)
        act.wait_ge(self.qk_p3, n - 1 + self.P3_0)
        act.wait_ge(self.qk_store[par], (n >> 1) * 48 + self.STORE0)
        for x in range(2):
            c = 2 * (k % 2) + x
            act.activation(self.full[par][:, x, :], self.qk_bank[par][:, x * 2 * P:(x + 1) * 2 * P], ACT.Identity,
                           bias=self.ln[:, 2 * i + 1, c:c + 1], scale=self.ln[:, 2 * i, c:c + 1]).then_inc(self.qk_full, 1)
        act.wait_ge(self.qk_full, 2 * n + 2 + self.FULL0)
        act.activation(self.part[0][par][:, :, :], self.full[par][:, :, :], ACT.Copy).then_inc(self.qk_p1, 1)

    def gpsimd(self, pool, n, par, k, pair):
        pool.wait_ge(self.qk_p1, n + 1)
        pool.tensor_tensor(self.rest[par][:, :, :], self.full[par][:, :, :], self.part[0][par][:, :, :],
                           ALU.subtract).then_inc(self.qk_rest, 1)
        pool.wait_ge(self.qk_p2, n + 1)
        pool.tensor_tensor(self.part[2][par][:, :, :], self.rest[par][:, :, :], self.part[1][par][:, :, :],
                           ALU.subtract).then_inc(self.qk_p3, 1)

    def vector(self, v, n, par, k, pair):
        v.wait_ge(self.qk_rest, n + 1)
        v.tensor_copy(self.part[1][par][:, :, :], self.rest[par][:, :, :]).then_inc(self.qk_p2, 1)

    def sync(self, sp, n, par, k, pair):
        t, c0 = "qk"[k // 2], 2 * (k % 2)
        row, tok = (n >> 4) % B, (n >> 2) % 4
        for x, (ready, start) in enumerate(((self.qk_p1, 0), (self.qk_p2, 0), (self.qk_p3, self.P3_0))):
            sp.wait_ge(ready, n + 1 + start)
            dst = self.scratch[t, x][bass.ds(row, 1), c0 * P:(c0 + 2) * P, bass.ds(tok * 2 * P, 2 * P)]
            sp.dma_start(dst.rearrange("a (c p) t -> p (a c) t", p=P), self.part[x][par][:, :, :])\
              .then_inc(self.qk_store[par], 16)

    def last_pair(self, k):
        return (TILES // 2 - 1) * self.UP + k, k % 2, k, 1

    def stored(self, sp, tiles):
        for par in range(2):
            sp.wait_ge(self.qk_store[par], tiles * 48 + self.STORE0)


class QuadLoads:
    SEM = 16 * 2 * (len(TERMS) + 1)

    def __init__(self, sem, scratch, alibi, ones):
        self.scratch, self.alibi, self.ones = scratch, alibi.bitcast(BF16), ones
        self.loaded = [sem(f"qk_loaded{i}") for i in range(BUFS)]
        self.ones_in = sem("ones_in")
        self.ones_set = sem("ones_set")

    def load(self, sp, n, s, q, k):
        for tile, t in ((k, 1), (q, 0)):
            sp.dma_start(tile[0:N_ALIBI, :, :], self.alibi[t].rearrange("(m h) r s -> m r h s", h=QH)[bass.ds(n % (H // QH), 1)]
                         .rearrange("a r h s -> (a r) h s")).then_inc(self.loaded[s], 16)
            for j, term in enumerate(TERMS):
                src = self.scratch["qk"[t], term[t]].rearrange("b (m h d) s -> (b m) d h s", h=QH, d=HD)
                r0 = R_DOT + HD * j
                sp.dma_start(tile[r0:r0 + HD, :, :], src[bass.ds(n, 1)].rearrange("a d h s -> (a d) h s"))\
                  .then_inc(self.loaded[s], 16)

    def load_ones(self, sp, k):
        sp.dma_start(k[R_MAX:K_EXP, :, :], self.ones[:, :].unsqueeze(1).broadcast_to([PARTS, QH, S])).then_inc(self.ones_in, 16)


def project_stage(nc, sem, bank, score_t, turner, quad_in, v_all, z_all, ident, ident_b, mask_b, qT0, kT0, ones,
                  x_in, w_qkv, q_w, q_b, k_w, k_b, lora_a, lora_b, ffn_w, ffn_bias, lora_w):
    WG = 4
    with ExitStack() as ctx:
        sb = lambda name, shape, dt: ctx.enter_context(nc.sbuf_tensor(name, shape, dt))
        wt_hi = sb("wt_hi", [P, DC, WG * D], F32R)
        wt_lo = sb("wt_lo", [P, DC, WG * D], F32R)
        w_raw = [qT0[:, :, :].bitcast(F32), kT0[:, :, :].bitcast(F32)]
        w_raw += [turner.qk[i][:, :, :, :].rearrange("p a b d -> p (a b) d") for i in range(2)]
        xt = sb("xt", [P, GT, D], F32)
        xT_hi = [sb(f"xT_hi{i}", [P, DC, P], F32R) for i in range(2)]
        xT_lo = [sb(f"xT_lo{i}", [P, DC, P], F32R) for i in range(2)]
        ln_rows = sb("ln_rows", [4 * DC, P], F32)
        qk, qk_norm = turner.qk, turner.qk_norm
        bias_bc = sb("bias_bc", [P, D], F32)
        la = sb("la", [P, D], F32)
        lb = sb("lb", [P, DC, NR * LR], F32)
        lbt = sb("lbt", [P, D], F32)
        lwb = sb("lwb", [P, NR], F32)
        eps = sb("eps", [P, 1], F32)
        st = sb("st", [P, 3, 6], F32)
        mv = sb("mv", [P, 3, 2], F32)
        sd = sb("sd", [P, 3], F32)
        rs = sb("rs", [P, 3], F32)

        consts = sem("consts")
        x_in_sem = [sem(f"x_loaded{i}") for i in range(GT)]
        w_in_sem = [sem(f"w_loaded{i}") for i in range(WG)]
        lora_in = sem("lora_loaded")
        small_in = sem("small_loaded")
        lb_scaled = sem("lora_b_scaled")
        ln_turned = sem("ln_turned")
        ln_scaled = sem("ln_scaled")
        lb_turned = sem("lora_b_turned")
        lbt_ready = sem("lora_bt_ready")
        w_turned = sem("w_turned")
        w_hi_done = sem("w_hi_done")
        w_lo_done = sem("w_lo_done")
        x_stat = sem("x_stat")
        x_sd = sem("x_sd")
        x_norm = sem("x_norm")
        x_turned = sem("x_turned")
        x_hi = sem("x_hi")
        x_lo = sem("x_lo")
        q_out = sem("q_out")
        k_out = sem("k_out")
        v_out = sem("v_out")
        z_out = sem("z_out")
        qk_clip = sem("qk_clip")
        v_done = sem("v_done")
        z_done = sem("z_done")
        qk_stat = sem("qk_stat")
        qk_sd = sem("qk_sd")
        waited = sem("waited")
        dve = sem("dve_chain")
        turn_bank = [bank[0], bank[1]]
        out_bank = [score_t[:, i, :] for i in range(4)]
        prep_bank = [bank[2], bank[3]] + out_bank
        xr = x_in.rearrange("b (t p) d -> (b t) p d", p=P)
        w_src = [w_qkv[g * D:(g + 1) * D, :] for g in range(3)] + [ffn_w]
        UP = turner.UP
        LORA, SMALL = 16 * (1 + DC + 1), 16 * 5
        PREP = len(prep_bank)
        vt = v_all[:, :, :, :].rearrange("p (b m) k f -> p b m k f", b=B)

        def groups(eng, body):
            body(0, True, False)
            with eng.Fori(1, GROUPS - 1) as g:
                body(g, False, False)
            body(GROUPS - 1, False, True)

        def units(g, t, first, unit):
            if not (first and t < 2):
                for x in range(2):
                    k = 2 * (t % 2) + x
                    unit((g * 2 + t // 2 - 1) * UP + k, k % 2, k, 1 - t // 2)

        with nc.Block() as block:
            @block.sync
            def _(sp):
                def load_w(g):
                    sp.dma_start(w_raw[g], w_src[g].rearrange("(t p) d -> p t d", p=P)).then_inc(w_in_sem[g], 16)

                def load_x(t):
                    sp.dma_start(xt[:, t, :], xr[t]).then_inc(x_in_sem[t], 16)

                load_w(0)
                load_x(0)
                load_w(1)
                for t in range(DC):
                    sp.dma_start(lb[:, t, :].rearrange("p (n r) -> p n r", n=NR),
                                 lora_b[:, t * P:(t + 1) * P, :].rearrange("n p r -> p n r")).then_inc(lora_in, 16)
                sp.dma_start(lwb[:, :], lora_w.rearrange("(a n) -> a n", a=1).broadcast_to([P, NR])).then_inc(lora_in, 16)
                sp.dma_start(la[:, :], lora_a.rearrange("n r d -> (n r) d")).then_inc(lora_in, 16)
                load_w(2)
                load_w(3)
                load_x(1)
                sp.dma_start(bias_bc[:, :], ffn_bias.rearrange("(a n) -> a n", a=1).broadcast_to([P, D])).then_inc(small_in, 16)
                for i, row in enumerate((q_w, q_b, k_w, k_b)):
                    sp.dma_start(ln_rows[i * DC:(i + 1) * DC, :], row.rearrange("(c p) -> c p", p=P)).then_inc(small_in, 16)
                load_x(2)
                load_x(3)

                def body(g, first, last):
                    for t in range(GT):
                        if not last:
                            sp.wait_ge(x_turned, g * GT + t + 1)
                            sp.dma_start(xt[:, t, :], xr[bass.ds(g * GT + GT + t, 1)].rearrange("a p d -> (a p) d")).then_inc(x_in_sem[t], 16)
                        units(g, t, first, lambda *unit: turner.sync(sp, *unit))
                        if last and t == 1:
                            turner.stored(sp, SB)
                            sp.wait_ge(w_turned, 2 * DC)
                            quad_in.load(sp, 0, 0, qT0, kT0)
                            sp.wait_ge(quad_in.ones_set, 1)
                            quad_in.load_ones(sp, kT0)
                groups(sp, body)

            @block.gpsimd
            def _(pool):
                pool.memset(eps[:, :], LN_EPS).then_inc(consts, 1)
                for m, v in ((ident, 0.0), (ident_b, 0.0), (mask_b, 0.0)):
                    pool.memset(m[:, :], v).then_inc(consts, 1)
                pool.wait_ge(consts, 4)
                for m in (ident, ident_b):
                    pool.affine_select(out=m[:, :], in_=m[:, :], compare_op=ALU.not_equal, fill=1.0, base=0,
                                       pattern=[[-1, P]], channel_multiplier=1).then_inc(consts, 1)
                pool.affine_select(out=mask_b[:, :], in_=mask_b[:, :], compare_op=ALU.is_ge, fill=MASKED, base=0,
                                   pattern=[[-1, P]], channel_multiplier=1).then_inc(consts, 1)
                pool.memset(ones[:, :], 1.0).then_inc(quad_in.ones_set, 1)
                pool.sem_inc(turner.qk_p3, turner.P3_0)
                for i in range(2):
                    pool.sem_inc(turner.qk_store[i], turner.STORE0)

                def body(g, first, last):
                    for t in range(GT):
                        units(g, t, first, lambda *unit: turner.gpsimd(pool, *unit))
                groups(pool, body)

            @block.scalar
            def _(act):
                act.sem_inc(turner.qk_full, turner.FULL0)

                def weights_hi(g):
                    for n in range(g * DC, (g + 1) * DC):
                        act.wait_ge(w_turned, n + 1)
                        act.activation(wt_hi[:, n % DC, g * D:(g + 1) * D], prep_bank[n % PREP][:, :], ACT.Copy).then_inc(w_hi_done, 1)

                def x_deviation(n):
                    act.wait_ge(x_stat, n + 1)
                    act.activation(sd[:, 2:3], mv[:, 2, 1:2], ACT.Sqrt, bias=eps[:, 0:1]).then_inc(x_sd, 1)

                def x_split(n, par):
                    act.wait_ge(x_turned, n + 1)
                    act.activation(xT_hi[par][:, :, :], turn_bank[par][:, :].rearrange("p (c t) -> p c t", c=DC),
                                   ACT.Copy).then_inc(x_hi, 1)

                act.wait_ge(consts, 1)
                act.activation(sd[:, 0:1], eps[:, 0:1], ACT.Sqrt)
                weights_hi(0)
                x_deviation(0)
                weights_hi(1)
                weights_hi(2)
                x_split(0, 0)
                weights_hi(3)
                act.wait_ge(ln_scaled, 1)

                def body(g, first, last):
                    for t in range(GT):
                        n = g * GT + t
                        nxt = not (last and t == GT - 1)
                        if nxt:
                            x_deviation(n + 1)
                        units(g, t, first, lambda *unit: turner.scalar(act, *unit))
                        act.wait_ge(qk_stat, n + 1)
                        act.activation(sd[:, 0:2], mv[:, 0:2, 1], ACT.Sqrt, bias=eps[:, 0:1]).then_inc(qk_sd, 1)
                        if nxt:
                            x_split(n + 1, (t + 1) % 2)
                groups(act, body)

            @block.tensor
            def _(pe):
                pe.wait_ge(consts, 7)

                def turn_weights(n):
                    g, dc = n // DC, n % DC
                    if dc == 0:
                        pe.wait_ge(w_in_sem[g], 16)
                    if n >= PREP:
                        pe.wait_ge(w_lo_done, n - PREP + 1)
                    dst = prep_bank[n % PREP]
                    if g < 3:
                        for t in range(4):
                            mm = pe.transpose(dst[:, t * P:(t + 1) * P], w_raw[g][:, t, dc * P:(dc + 1) * P], ident[:, :])
                    else:
                        pe.wait_ge(lbt_ready, 1)
                        pe.matmul(dst[:, :], la[:, dc * P:(dc + 1) * P], lbt[:, :], start=True, stop=False)
                        for t in range(4):
                            mm = pe.matmul(dst[:, t * P:(t + 1) * P], w_raw[g][:, t, dc * P:(dc + 1) * P], ident[:, :],
                                           start=False, stop=(t == 3))
                    mm.then_inc(w_turned, 1)

                def turn_x(n, t):
                    pe.wait_ge(x_norm, n + 1)
                    for c in range(DC):
                        mm = pe.transpose(turn_bank[t % 2][:, c * P:(c + 1) * P], xt[:, t, c * P:(c + 1) * P], ident[:, :])
                    mm.then_inc(x_turned, 1)

                def project(n, t, which, signal):
                    wcols = slice(which * D, (which + 1) * D)
                    terms = [(xT_hi, wt_hi), (xT_hi, wt_lo), (xT_lo, wt_hi)]
                    for j, (a, w) in enumerate(terms):
                        for c in range(DC):
                            mm = pe.matmul(out_bank[which], a[t % 2][:, c, :], w[:, c, wcols],
                                           start=(j == 0 and c == 0), stop=(j == 2 and c == DC - 1))
                    mm.then_inc(signal, 1)

                for n in range(2 * DC):
                    turn_weights(n)
                pe.wait_ge(lb_scaled, 1)
                for t in range(DC):
                    mm = pe.transpose(turn_bank[1][:, t * P:(t + 1) * P], lb[:, t, :], ident[:, :])
                mm.then_inc(lb_turned, 1)
                for n in range(2 * DC, 3 * DC):
                    turn_weights(n)
                turn_x(0, 0)
                for n in range(3 * DC, WG * DC):
                    turn_weights(n)
                pe.wait_ge(small_in, SMALL)
                pe.wait_ge(lbt_ready, 1)
                pe.transpose(turn_bank[1][:, 0:4 * DC], ln_rows[:, :], ident[0:4 * DC, 0:4 * DC]).then_inc(ln_turned, 1)
                pe.wait_ge(w_lo_done, WG * DC)

                def body(g, first, last):
                    for t in range(GT):
                        n = g * GT + t
                        todo = []
                        units(g, t, first, lambda *args: todo.append(args))
                        pe.wait_ge(x_hi, n + 1)
                        pe.wait_ge(x_lo, n + 1)
                        pe.wait_ge(qk_clip, 2 * n + 1)
                        project(n, t, 0, q_out)
                        if todo:
                            turner.tensor(pe, *todo[0])
                        pe.wait_ge(qk_clip, 2 * n + 2)
                        project(n, t, 1, k_out)
                        if todo:
                            turner.tensor(pe, *todo[1])
                        pe.wait_ge(v_done, n + 1)
                        project(n, t, 2, v_out)
                        if not (last and t == GT - 1):
                            turn_x(n + 1, (t + 1) % GT)
                        pe.wait_ge(z_done, n + 1)
                        project(n, t, 3, z_out)
                groups(pe, body)

            @block.vector
            def _(v):
                v.sem_inc(qk_clip, 2)
                v.sem_inc(v_done, 1)
                v.sem_inc(z_done, 1)
                CHAIN = 5
                chained = [0]

                def chain(ins, base):
                    chained[0] += 1
                    ins.then_inc(dve, 1)
                    v.wait_ge(dve, base + chained[0])

                def stats(slot, src, base):
                    chain(v.bn_stats(st[:, slot, :], src), base)
                    v.sem_inc(waited, 1)
                    return v.bn_aggr(mv[:, slot, :], st[:, slot, :])

                def x_stats(t, k, base):
                    v.wait_ge(x_in_sem[t], 16 * k)
                    stats(2, xt[:, t, :], base).then_inc(x_stat, 1)

                def x_normalise(n, t, base):
                    v.wait_ge(x_sd, n + 1)
                    chain(v.reciprocal(rs[:, 2:3], sd[:, 2:3]), base)
                    v.tensor_scalar(xt[:, t, :], xt[:, t, :], mv[:, 2, 0:1], rs[:, 2:3], ALU.subtract, ALU.mult).then_inc(x_norm, 1)

                def x_split(n, par):
                    v.wait_ge(x_hi, n + 1)
                    v.tensor_tensor(xT_lo[par][:, :, :], turn_bank[par][:, :].rearrange("p (c t) -> p c t", c=DC),
                                    xT_hi[par][:, :, :].bitcast(F32), ALU.subtract).then_inc(x_lo, 1)

                def weights_lo(g):
                    for n in range(g * DC, (g + 1) * DC):
                        v.wait_ge(w_hi_done, n + 1)
                        v.tensor_tensor(wt_lo[:, n % DC, g * D:(g + 1) * D], prep_bank[n % PREP][:, :],
                                        wt_hi[:, n % DC, g * D:(g + 1) * D].bitcast(F32), ALU.subtract).then_inc(w_lo_done, 1)

                weights_lo(0)
                x_stats(0, 1, 0)
                v.wait_ge(lora_in, LORA)
                for t in range(DC):
                    lbv = lb[:, t, :].rearrange("p (n r) -> p n r", n=NR)
                    ins = v.tensor_tensor(lbv, lbv, lwb[:, :].unsqueeze(2).broadcast_to([P, NR, LR]), ALU.mult)
                ins.then_inc(lb_scaled, 1)
                weights_lo(1)
                x_normalise(0, 0, 0)
                v.wait_ge(lb_turned, 1)
                v.tensor_scalar(lbt[:, :], turn_bank[1][:, :], LORA_SCALE, None, ALU.mult).then_inc(lbt_ready, 1)
                weights_lo(2)
                x_split(0, 0)
                weights_lo(3)
                v.wait_ge(ln_turned, 1)
                for i, scale in enumerate((HD ** -0.5, 1.0)):
                    ins = v.tensor_scalar(turner.ln[:, 2 * i:2 * i + 2, :],
                                          turn_bank[1][:, 2 * i * DC:2 * (i + 1) * DC].rearrange("p (a c) -> p a c", c=DC),
                                          scale, None, ALU.mult)
                ins.then_inc(ln_scaled, 1)
                v.wait_ge(small_in, SMALL)
                before = chained[0]

                def body(g, first, last):
                    for t in range(GT):
                        n = g * GT + t
                        nxt = not (last and t == GT - 1)
                        base = n * CHAIN + before
                        todo = []
                        units(g, t, first, lambda *args: todo.append(args))
                        pair = qk[t // 2]
                        chained[0] = 0
                        if nxt:
                            x_stats((t + 1) % GT, g + 1 + (t + 1) // GT, base)
                        for i, ready in ((0, q_out), (1, k_out)):
                            v.wait_ge(ready, n + 1)
                            v.tensor_scalar(pair[:, i, t % 2, :], out_bank[i], -CLIP, CLIP, ALU.max, ALU.min).then_inc(qk_clip, 1)
                            v.wait_ge(qk_clip, 2 * n + i + 3)
                            agg = stats(i, pair[:, i, t % 2, :], base)
                            if i:
                                agg.then_inc(qk_stat, 1)
                            if i == 0 and nxt:
                                x_normalise(n + 1, (t + 1) % GT, base)
                            if todo:
                                turner.vector(v, *todo[i])
                        v.wait_ge(v_out, n + 1)
                        half = g >> 1
                        dst = vt[:, bass.ds(half, 1), :, bass.ds((g % 2) * GT + t, 1), :].rearrange("p a m k f -> p (a m k) f")
                        v.tensor_scalar(dst, out_bank[2].rearrange("p (m f) -> p m f", f=QH * HD), -CLIP, CLIP,
                                        ALU.max, ALU.min).then_inc(v_done, 1)
                        if nxt:
                            x_split(n + 1, (t + 1) % 2)
                        v.wait_ge(qk_sd, n + 1)
                        chain(v.reciprocal(rs[:, 0:2], sd[:, 0:2]), base)
                        for i in range(2):
                            ins = v.tensor_scalar(pair[:, i, t % 2, :], pair[:, i, t % 2, :], mv[:, i, 0:1], rs[:, i:i + 1],
                                                  ALU.subtract, ALU.mult)
                        ins.then_inc(qk_norm, 1)
                        v.wait_ge(z_out, n + 1)
                        v.tensor_tensor(z_all[:, bass.ds(n, 1), :].rearrange("p a d -> p (a d)"), out_bank[3], bias_bc[:, :],
                                        ALU.add).then_inc(z_done, 1)
                groups(v, body)


def attend_stage(nc, sem, bank, score_t, turner, quad_in, qT0, kT0, v_all, ident, ident_b, mask_b, attn, w_out, wo_hi, wo_lo, stage):
    with ExitStack() as ctx:
        sb = lambda name, shape, dt: ctx.enter_context(nc.sbuf_tensor(name, shape, dt))
        qT = [qT0] + [sb(f"qT{i}", [P, QH, S], BF16) for i in range(1, BUFS)]
        kT = [kT0] + [sb(f"kT{i}", [P, QH, S], BF16) for i in range(1, BUFS)]
        vq = [sb(f"vq{i}", [P, SB, QH, 32], F32) for i in range(BUFS)]
        prob = [sb(f"prob{i}", [P, QH, CW], F32) for i in range(3)]
        oT = [sb(f"oT{i}", [P, CW], F32) for i in range(2)]
        top = sb("top", [P, 2, SB, QH], F32)
        mrest = sb("mrest", [P, 4, QH], F32)
        msplit = [sb(f"msplit{i}", [P, 4, QH, PARTS], BF16) for i in range(2)]
        mrow = [sb(f"mrow{i}", [QH * PARTS, CW], BF16) for i in range(2)]
        inv = sb("inv", [P, 4, QH], F32)
        warm = sb("warm", [P, 1], F32)
        wo_raw = turner.qk[0][:, :, :, :].rearrange("p a b d -> p (a b) d")

        score_q = [bank[0], bank[1]]
        score_ring = score_q + [score_t[:, i, :] for i in range(4)]
        out_t = bank[2]
        turn = bank[3]
        turn_b = turn[:, :].bitcast(BF16)

        loaded, LOADS = quad_in.loaded, quad_in.SEM
        quad_free = sem("quad_free")
        v_copied = sem("v_copied")
        piece_out = sem("piece_out")
        piece_max = sem("piece_max")
        top_done = sem("top_done")
        m_split = [sem(f"m_split{c}") for c in range(2)]
        m_chain = sem("m_chain")
        v_filled = sem("v_filled")
        turned = sem("turned")
        turn_free = sem("turn_free")
        m_rows = [sem(f"m_rows{c}") for c in range(2)]
        m_in = [sem(f"m_in{c}") for c in range(2)]
        st_out = sem("st_out")
        exp_done = sem("exp_done")
        pv_done = sem("pv_done")
        o_taken = sem("o_taken")
        inv_done = sem("inv_done")
        wo_in = sem("wo_loaded")
        wo_turned = sem("wo_turned")
        wo_hi_done = sem("wo_hi_done")
        wo_lo_done = sem("wo_lo_done")
        HU = 2 * NU
        turn_after = {0: 0, 1: 1, 8: 2, 22: 3}
        part_after = {6: 0, 11: 1, 24: 2, 31: 3}
        EXP0, PIECE0, PV0, FREE0, ROWS0, TURN0 = 2, 6, 3, 2, 64, 1

        wo_unit = {1: 0, 3: 1, 5: 2, 7: 3}

        def quads(eng, step):
            with eng.Fori(0, QUADS // BUFS - 1) as i:
                for s in range(BUFS):
                    step(i * BUFS + s, s, i, BUFS)
            for n in range(QUADS - QUADS % BUFS - BUFS, QUADS):
                step(n, n % BUFS, n // BUFS, QUADS - 1 - n)

        with nc.Block() as block:
            @block.sync
            def _(sp):
                def send_rows(s, c):
                    for h in range(QH):
                        sp.dma_start(qT[s][R_MAX:K_EXP, h, c * CW:(c + 1) * CW], mrow[c][PARTS * h:PARTS * (h + 1), :])\
                          .then_inc(m_in[c], 16)

                for k in range(2):
                    turner.sync(sp, *turner.last_pair(k))
                quad_in.load(sp, 1, 1, qT[1], kT[1])
                for s in range(1, BUFS):
                    quad_in.load_ones(sp, kT[s])
                sp.wait_ge(m_rows[0], 1)
                send_rows(0, 0)
                for k in range(2, turner.UP):
                    turner.sync(sp, *turner.last_pair(k))
                turner.stored(sp, TILES)
                sp.dma_start(wo_raw[:, :, :], w_out.rearrange("(t p) d -> p t d", p=P)).then_inc(wo_in, 16)

                def step(n, s, i, left):
                    sp.wait_ge(m_rows[1], n + 1)
                    send_rows(s, 1)
                    if left >= 2:
                        sp.wait_ge(quad_free, n + FREE0)
                        nxt = (s + 2) % BUFS
                        quad_in.load(sp, n + 2, nxt, qT[nxt], kT[nxt])
                    if left >= 1:
                        sp.wait_ge(m_rows[0], n + 2)
                        send_rows((s + 1) % BUFS, 0)
                quads(sp, step)
                sp.wait_ge(m_in[0], 64 * QUADS)
                sp.wait_ge(m_in[1], 64 * QUADS + ROWS0)

            @block.gpsimd
            def _(pool):
                pool.sem_inc(m_in[1], ROWS0)
                for k in range(2):
                    turner.gpsimd(pool, *turner.last_pair(k))
                for i in range(BUFS):
                    pool.memset(vq[i][:, :, :, :], 1.0).then_inc(v_filled, 1)
                pool.wait_ge(v_filled, BUFS)

                def copy_v(n, s):
                    pool.tensor_copy(vq[s][:, :, :, 0:HD], v_all[:, bass.ds(n, 1), :, :]
                                     .rearrange("p a k (h d) -> p (a k) h d", h=QH)).then_inc(v_copied, 1)

                copy_v(0, 0)
                for k in range(2, turner.UP):
                    turner.gpsimd(pool, *turner.last_pair(k))

                def step(n, s, i, left):
                    if left:
                        pool.wait_ge(quad_free, n - 1 + FREE0)
                        copy_v(n + 1, (s + 1) % BUFS)
                    else:
                        pool.wait_ge(turn_free, 2 * (QUADS // B) + TURN0)
                        stage(pool, 0, 0, 0)
                quads(pool, step)

            @block.scalar
            def _(act):
                act.sem_inc(exp_done, EXP0)

                def maxima_rows(c, wait_rows, use):
                    act.wait_ge(turned, use)
                    if wait_rows is not None:
                        act.wait_ge(m_in[c], wait_rows)
                    act.activation(mrow[c][:, :], turn_b[0:QH * PARTS, 0:CW], ACT.Copy).then_inc(m_rows[c], 1)

                for k in range(turner.UP):
                    if k == 2:
                        maxima_rows(0, None, 1)
                    turner.scalar(act, *turner.last_pair(k))

                act.activation(warm[:, :], ident[:, 0:1], ACT.Exp)

                def take_output(n, c):
                    last_unit = 4 * (c + 1) - 1 if c == 0 else NU - 1
                    act.wait_ge(pv_done, n * NU + last_unit + 1 + PV0)
                    act.activation(oT[c][:, :], out_t[:, :], ACT.Copy).then_inc(o_taken, 1)

                def step(n, s, i, left):
                    for u, (c, kb) in enumerate(UNITS):
                        _, w = unit_cols(c, kb)
                        for j in range(2):
                            act.wait_ge(st_out, n * HU + 2 * u + j + 1)
                            if j == 0:
                                act.wait_ge(pv_done, n * NU + u - 2 + PV0)
                            act.activation(prob[u % 3][:, 2 * j:2 * j + 2, 0:w], score_t[:, 2 * j:2 * j + 2, 0:w],
                                           ACT.Exp).then_inc(exp_done, 1)
                        if left == 0 and u in wo_unit:
                            dc = wo_unit[u]
                            act.wait_ge(wo_turned, dc + 1)
                            act.activation(wo_hi[:, dc, :], score_q[dc % 2][:, :], ACT.Copy).then_inc(wo_hi_done, 1)
                        if u == U_M1:
                            maxima_rows(1, n * 64 + ROWS0, n * 4 + 2)
                        if u == U_M0 and left:
                            maxima_rows(0, n * 64 + 64, n * 4 + 3)
                        if u == 4:
                            take_output(n, 0)
                    take_output(n, 1)
                quads(act, step)

            @block.tensor
            def _(pe):
                pe.sem_inc(pv_done, PV0)
                pe.sem_inc(quad_free, FREE0)

                def piece(q, s, p, ring=score_q):
                    qb, kc, h0, nh, w = PIECES[p]
                    pe.wait_ge(piece_max, q * NP + p + 1 - len(ring) + PIECE0)
                    dst = ring[p % len(ring)]
                    for x in range(nh):
                        h = h0 + x
                        mm = pe.matmul(dst[:, x * w:(x + 1) * w], qT[s][0:K_MAX, h, qb * P:(qb + 1) * P],
                                       kT[s][0:K_MAX, h, kc * CW:kc * CW + w], start=True, stop=(kc != qb // 4))
                        if kc == qb // 4:
                            mm = pe.matmul(dst[:, (x + 1) * w - P:(x + 1) * w], ident_b[:, :], mask_b[:, :],
                                           start=False, stop=True)
                    mm.then_inc(piece_out, 1)

                def turn_maxima(c, q):
                    pe.wait_ge(m_split[c], q + 1)
                    for b in range(4):
                        mm = pe.transpose(turn_b[0:QH * PARTS, b * P:(b + 1) * P],
                                          msplit[c][:, b, :, :].rearrange("p h x -> p (h x)"), ident_b[:, :])
                    mm.then_inc(turned, 1)

                def turn_output(n, c):
                    pe.wait_ge(o_taken, 2 * n + c + 1)
                    for b in range(4):
                        mm = pe.transpose(turn[:, b * P:(b + 1) * P], oT[c][:, b * P:(b + 1) * P], ident[:, :])
                        if c == 1 and b == 0:
                            mm.then_inc(quad_free, 1)
                    mm.then_inc(turned, 1)

                def exponents(n, s, u, j):
                    c, kb = UNITS[u]
                    q0, w = unit_cols(c, kb)
                    pe.wait_ge(exp_done, n * HU + 2 * u + j - 1 + EXP0)
                    for h in range(2 * j, 2 * j + 2):
                        mm = pe.matmul(score_t[:, h, 0:w], kT[s][0:K_EXP, h, kb * P:(kb + 1) * P],
                                       qT[s][0:K_EXP, h, q0:q0 + w], start=True, stop=not is_diag(c, kb))
                        if is_diag(c, kb):
                            mm = pe.matmul(score_t[:, h, 0:P], mask_b[:, :], ident_b[:, :], start=False, stop=True)
                    mm.then_inc(st_out, 1)

                def apply_v(n, s, u):
                    c, kb = UNITS[u]
                    q0, w = unit_cols(c, kb)
                    pe.wait_ge(exp_done, n * HU + 2 * u + 2 + EXP0)
                    for h in range(QH):
                        mm = pe.matmul(out_t[32 * h:32 * h + 32, q0 - CW * c:q0 - CW * c + w], vq[s][:, kb, h, :],
                                       prob[u % 3][:, h, 0:w], start=(kb == 0), stop=(kb == 4 * (c + 1) - 1))
                    mm.then_inc(pv_done, 1)

                def turn_out_weights(dc):
                    if dc == 0:
                        pe.wait_ge(wo_in, 16)
                        pe.wait_ge(piece_max, QUADS * NP + PIECE0)
                    if dc >= 2:
                        pe.wait_ge(wo_lo_done, dc - 1)
                    for t in range(4):
                        mm = pe.transpose(score_q[dc % 2][:, t * P:(t + 1) * P], wo_raw[:, t, dc * P:(dc + 1) * P], ident[:, :])
                    mm.then_inc(wo_turned, 1)

                pe.wait_ge(loaded[0], LOADS)
                for p in range(NP):
                    piece(0, 0, p, score_ring)
                    if p in turn_after:
                        if turn_after[p] == 3:
                            pe.wait_ge(m_rows[0], 1)
                        turner.tensor(pe, *turner.last_pair(turn_after[p]))
                    if p == NP0 + 3:
                        pe.wait_ge(turner.qk_full, turner.UP * TILES - 4 + turner.FULL0)
                        turn_maxima(0, 0)
                pe.wait_ge(turner.qk_full, turner.UP * TILES + turner.FULL0)
                pe.wait_ge(quad_in.ones_in, 16 * BUFS)

                def first_exponents(n, s):
                    pe.wait_ge(m_in[0], n * 64 + 64)
                    for j in range(2):
                        exponents(n, s, 0, j)

                assert [p % len(score_ring) for p in range(NP)][-2:] == [0, 1]
                pe.wait_ge(piece_max, NP - 2 + PIECE0)
                first_exponents(0, 0)

                def step(n, s, i, left):
                    pe.wait_ge(v_copied, n + 1)
                    nxt = (s + 1) % BUFS

                    def pieces(slot):
                        if left:
                            for p in slot_pieces(slot):
                                piece(n + 1, nxt, p)

                    for u in range(NU):
                        if UNITS[u] == (1, 0):
                            pe.wait_ge(m_in[1], n * 64 + 64 + ROWS0)
                        if u:
                            exponents(n, s, u, 0)
                        elif left:
                            pe.wait_ge(loaded[nxt], (i + 1 + (s + 1) // BUFS) * LOADS)
                        pieces(3 * u)
                        if u:
                            exponents(n, s, u, 1)
                        pieces(3 * u + 1)
                        if left == 0 and u in wo_unit:
                            turn_out_weights(wo_unit[u])
                        if u == U_M1:
                            pe.wait_ge(m_rows[0], n + 1)
                            pe.wait_ge(turn_free, n * 2 + TURN0)
                            turn_maxima(1, n)
                        if u == U_M0 and left:
                            pe.wait_ge(m_rows[1], n + 1)
                            turn_maxima(0, n + 1)
                        if u >= 1:
                            if u == 5:
                                pe.wait_ge(o_taken, 2 * n + 1)
                            apply_v(n, s, u - 1)
                        pieces(3 * u + 2)
                        if u == U_O0:
                            if left:
                                pe.wait_ge(m_rows[0], n + 2)
                            else:
                                pe.wait_ge(m_rows[1], n + 1)
                            turn_output(n, 0)
                    apply_v(n, s, NU - 1)
                    pieces(3 * NU)
                    if left:
                        first_exponents(n + 1, nxt)
                    pe.wait_ge(turn_free, n * 2 + 1 + TURN0)
                    turn_output(n, 1)
                quads(pe, step)

            @block.vector
            def _(v):
                v.sem_inc(piece_max, PIECE0)
                v.sem_inc(turn_free, TURN0)

                def maxima(q, p, ring=score_q):
                    qb, kc, h0, nh, w = PIECES[p]
                    v.wait_ge(piece_out, q * NP + p + 1)
                    v.tensor_reduce(top[:, kc, qb, h0:h0 + nh], ring[p % len(ring)][:, 0:nh * w].rearrange("p (h w) -> p h w", w=w),
                                    AX.X, ALU.max).then_inc(piece_max, 1)

                def split(q, c, pieces):
                    v.wait_ge(piece_max, q * NP + pieces + PIECE0)
                    if c == 1:
                        v.tensor_tensor(top[:, 0, 4:8, :], top[:, 0, 4:8, :], top[:, 1, 4:8, :], ALU.max).then_inc(top_done, 1)
                        v.wait_ge(top_done, q + 1)
                    m = top[:, 0, 4 * c:4 * c + 4, :]
                    one, two, three = (msplit[c][:, :, :, x] for x in range(PARTS))
                    v.tensor_scalar(one, m, -1.0, None, ALU.mult).then_inc(m_chain, 1)
                    k = (2 * q + c) * 3
                    v.wait_ge(m_chain, k + 1)
                    v.scalar_tensor_tensor(out=mrest[:, :, :], in0=m, scalar=-1.0, in1=one, op0=ALU.mult, op1=ALU.subtract)\
                     .then_inc(m_chain, 1)
                    v.wait_ge(m_chain, k + 2)
                    v.tensor_copy(two, mrest[:, :, :]).then_inc(m_chain, 1)
                    v.wait_ge(m_chain, k + 3)
                    v.tensor_tensor(three, mrest[:, :, :], two, ALU.subtract).then_inc(m_split[c], 1)

                def normalise(n, c, use):
                    v.wait_ge(turned, use)
                    o = turn[:, :].rearrange("p (b h x) -> p b h x", b=4, h=QH)
                    v.reciprocal(inv[:, :, :], o[:, :, :, HD]).then_inc(inv_done, 1)
                    v.wait_ge(inv_done, 2 * n + c + 1)
                    dst = attn[:, bass.ds(n, 1), 4 * c:4 * c + 4, :].rearrange("p a b (h d) -> p (a b) h d", h=QH)
                    v.tensor_tensor(dst, o[:, :, :, 0:HD], inv[:, :, :].unsqueeze(3).broadcast_to([P, 4, QH, HD]),
                                    ALU.mult).then_inc(turn_free, 1)

                for p in range(NP):
                    maxima(0, p, score_ring)
                    if p in part_after:
                        turner.vector(v, *turner.last_pair(part_after[p]))
                    if p == NP0 - 1:
                        split(0, 0, NP0)
                split(0, 1, NP)

                def step(n, s, i, left):
                    def pieces(slot):
                        if left:
                            for p in slot_pieces(slot):
                                maxima(n + 1, p)
                                if p == NP0 - 1:
                                    split(n + 1, 0, NP0)

                    for u in range(NU):
                        for k in range(3):
                            pieces(3 * u + k)
                        if left == 0 and u in wo_unit:
                            dc = wo_unit[u]
                            v.wait_ge(wo_hi_done, dc + 1)
                            v.tensor_tensor(wo_lo[:, dc, :], score_q[dc % 2][:, :], wo_hi[:, dc, :].bitcast(F32), ALU.subtract)\
                             .then_inc(wo_lo_done, 1)
                        if u == U_O0:
                            normalise(n, 0, n * 4 + (4 if left else 3))
                    pieces(3 * NU)
                    if left:
                        split(n + 1, 1, NP)
                    normalise(n, 1, n * 4 + (5 if left else 4))
                quads(v, step)


def combine_stage(nc, sem, bank, x_in, wo_hi, wo_lo, z_all, at, staged, stage, ident, out):
    with ExitStack() as ctx:
        sb = lambda name, shape, dt: ctx.enter_context(nc.sbuf_tensor(name, shape, dt))
        aT_hi = [sb(f"aT_hi{i}", [P, DC, P], F32R) for i in range(2)]
        aT_lo = [sb(f"aT_lo{i}", [P, DC, P], F32R) for i in range(2)]
        xc = [sb(f"xc{i}", [P, D], F32) for i in range(2)]
        gate = [sb(f"gate{i}", [P, D], F32) for i in range(2)]
        prod = [sb(f"prod{i}", [P, D], F32) for i in range(2)]
        y = [sb(f"y{i}", [P, D], F32) for i in range(2)]
        warm = sb("warm_silu", [P, 1], F32)
        turn_bank, out_bank = [bank[0], bank[1]], [bank[2], bank[3]]

        x_loaded = [sem(f"xc_loaded{i}") for i in range(2)]
        a_turned = sem("a_turned")
        a_hi = sem("a_hi")
        a_lo = sem("a_lo")
        projected = sem("projected")
        gated = sem("gated")
        multiplied = sem("multiplied")
        y_done = sem("y_done")
        y_stored = [sem(f"y_stored{i}") for i in range(2)]
        xr = x_in.rearrange("b (t p) d -> (b t) p d", p=P)
        yr = out.rearrange("b (t p) d -> (b t) p d", p=P)
        A0, Y0, MUL0 = 1, 2, 2

        def tiles(eng, step):
            with eng.Fori(0, TILES // TB - 1) as i:
                for t in range(TB):
                    step(i * TB + t, i, t, TB)
            i = TILES // TB - 1
            for t in range(TB):
                step(i * TB + t, i, t, TB - 1 - t)

        with nc.Block() as block:
            @block.sync
            def _(sp):
                for t in range(2):
                    sp.dma_start(xc[t][:, :], xr[t]).then_inc(x_loaded[t], 16)

                def step(n, i, t, left):
                    sp.wait_ge(y_done, n + 1 + Y0)
                    sp.dma_start(yr[bass.ds(n, 1)].rearrange("a p d -> (a p) d"), y[t % 2][:, :]).then_inc(y_stored[t % 2], 16)
                    if left >= 2:
                        sp.dma_start(xc[t % 2][:, :], xr[bass.ds(n + 2, 1)].rearrange("a p d -> (a p) d")).then_inc(x_loaded[t % 2], 16)
                tiles(sp, step)
                for t in range(2):
                    sp.wait_ge(y_stored[t], 16 * TILES // 2 + 16)

            @block.gpsimd
            def _(pool):
                def step(n, i, t, left):
                    if left:
                        pool.wait_ge(a_turned, n + A0)
                        stage(pool, n + 1, i + (t + 1) // TB, (t + 1) % TB)
                tiles(pool, step)

            @block.scalar
            def _(act):
                def cut(n, t):
                    act.wait_ge(a_turned, n + 1 + A0)
                    act.activation(aT_hi[t % 2][:, :, :], turn_bank[t % 2][:, :].rearrange("p (c t) -> p c t", c=DC),
                                   ACT.Copy).then_inc(a_hi, 1)

                cut(0, 0)

                def step(n, i, t, left):
                    act.wait_ge(y_done, n - 1 + Y0)
                    act.activation(gate[t % 2][:, :], z_all[:, bass.ds(n, 1), :].rearrange("p a d -> p (a d)"),
                                   ACT.Silu).then_inc(gated, 1)
                    if left:
                        cut(n + 1, t + 1)
                act.activation(warm[:, :], ident[:, 0:1], ACT.Silu)
                tiles(act, step)

            @block.tensor
            def _(pe):
                pe.sem_inc(a_turned, A0)

                def turn_tile(n, t):
                    pe.wait_ge(staged, n + 1)
                    for c in range(DC):
                        mm = pe.transpose(turn_bank[t % 2][:, c * P:(c + 1) * P], at[t % 2][:, c * P:(c + 1) * P], ident[:, :])
                    mm.then_inc(a_turned, 1)

                turn_tile(0, 0)

                def step(n, i, t, left):
                    if left:
                        turn_tile(n + 1, t + 1)
                    pe.wait_ge(a_hi, n + 1)
                    pe.wait_ge(a_lo, n + 1)
                    pe.wait_ge(multiplied, n - 1 + MUL0)
                    for j, (a, w) in enumerate([(aT_hi, wo_hi), (aT_hi, wo_lo), (aT_lo, wo_hi)]):
                        for c in range(DC):
                            mm = pe.matmul(out_bank[t % 2][:, :], a[t % 2][:, c, :], w[:, c, :],
                                           start=(j == 0 and c == 0), stop=(j == 2 and c == DC - 1))
                    mm.then_inc(projected, 1)
                tiles(pe, step)

            @block.vector
            def _(v):
                v.sem_inc(multiplied, MUL0)
                v.sem_inc(y_done, Y0)
                for t in range(2):
                    v.sem_inc(y_stored[t], 16)

                def cut(n, t):
                    v.wait_ge(a_hi, n + 1)
                    v.tensor_tensor(aT_lo[t % 2][:, :, :], turn_bank[t % 2][:, :].rearrange("p (c t) -> p c t", c=DC),
                                    aT_hi[t % 2][:, :, :].bitcast(F32), ALU.subtract).then_inc(a_lo, 1)

                cut(0, 0)

                def step(n, i, t, left):
                    if left:
                        cut(n + 1, t + 1)
                    v.wait_ge(projected, n + 1)
                    v.wait_ge(gated, n + 1)
                    v.tensor_tensor(prod[t % 2][:, :], out_bank[t % 2][:, :], gate[t % 2][:, :], ALU.mult).then_inc(multiplied, 1)
                    v.wait_ge(multiplied, n + 1 + MUL0)
                    v.wait_ge(x_loaded[t % 2], (i * 2 + t // 2) * 16 + 16)
                    v.wait_ge(y_stored[t % 2], (i * 2 + t // 2) * 16 + 16)
                    v.tensor_tensor(y[t % 2][:, :], prod[t % 2][:, :], xc[t % 2][:, :], ALU.add).then_inc(y_done, 1)
                tiles(v, step)


_INS = ['L0_attn_hidden_states', 'L0_attn_w_qkv', 'L0_attn_q_ln_w', 'L0_attn_q_ln_b', 'L0_attn_k_ln_w', 'L0_attn_k_ln_b',
        'L0_attn_w_out', 'L0_ffn_lora_A', 'L0_ffn_lora_B', 'L0_ffn_W', 'L0_ffn_bias', 'L0_ffn_lora_weights']


def alibi_rows():
    import numpy as _np
    slopes = (_np.float32(1.0) / _np.power(_np.float32(2.0), _np.arange(1, H + 1, dtype=_np.float32) * _np.float32(8 / H)))
    pos = _np.arange(S, dtype=_np.float32)
    one = _np.ones(S, _np.float32)
    rows = _np.empty((2, H, N_ALIBI, S), _np.float32)
    for h in range(H):
        left = _np.float32(slopes[h])
        for x in range(PARTS):
            s = (left.reshape(1).view(_np.uint32) & _np.uint32(0xFFFF0000)).view(_np.float32)[0]
            left = left - s
            for y, p in enumerate((pos - pos % P, pos % P)):
                r = 4 * x + 2 * y
                rows[0, h, r], rows[1, h, r] = s * one, p
                rows[0, h, r + 1], rows[1, h, r + 1] = -p, s * one
    return (rows.view(_np.uint32) >> 16).astype(_np.uint16)


def kernel(**inputs):
    import numpy as _np
    import concourse.bacc as _bacc
    from concourse import mybir as _mybir
    from concourse.bass_utils import run_bass_kernel_spmd as _run

    nc = _bacc.Bacc("TRN2", target_bir_lowering=False, num_devices=1)
    arrays, args = {}, []
    for name in _INS:
        a = _np.ascontiguousarray(inputs[name])
        arrays[f"in_{name}_dram"] = a
        args.append(nc.dram_tensor(f"in_{name}_dram", a.shape, _mybir.dt.from_np(a.dtype), kind="ExternalInput").ap())
    rows = alibi_rows()
    arrays["alibi_dram"] = rows
    args.append(nc.dram_tensor("alibi_dram", rows.shape, _mybir.dt.uint16, kind="ExternalInput").ap())
    args.append(nc.dram_tensor("out_0_dram", (B, S, D), _mybir.dt.float32, kind="ExternalOutput").ap())
    build(nc, *args)
    r = _run(nc, [arrays], core_ids=[0])
    return r.results[0]["out_0_dram"]
```
